# Optimizing a Trainium2 kernel written in Bass

```python
import numpy as np
import jax
import jax.numpy as jnp

def _softmax(x, axis=-1):
    return jax.nn.softmax(x, axis=axis)

def _gelu(x):
    return jax.nn.gelu(x, approximate=True)

def _silu(x):
    return jax.nn.silu(x)

def _sigmoid(x):
    return jax.nn.sigmoid(x)

def _layernorm(x, axis=-1, eps=1e-05):
    m = jnp.mean(x, axis=axis, keepdims=True)
    v = jnp.var(x, axis=axis, keepdims=True)
    return (x - m) / jnp.sqrt(v + eps)

def _scatter_add(tgt, idx, src, axis=0):
    return tgt.at[idx].add(src)

def _segment_sum(src, seg, n):
    return jax.ops.segment_sum(src, seg, n)
kernel_name = 'mk_xattn_seq_d4_seqx_r4_40e6aa'

def setup_inputs(seed: int=0):
    np.random.seed(seed)
    _w = jnp.asarray

    def _rec_inputs():
        import jax
        import jax.numpy as jnp
        _rk = jax.random.key(seed)
        x = 7.22e-05 + 1 * jax.random.normal(jax.random.fold_in(_rk, 1), (4, 512, 512), jnp.float32)
        _lenS = 512 - jax.random.randint(jax.random.fold_in(_rk, 7), (4,), 0, max(1, 512 // 4) + 1, jnp.int32)
        _lenS2 = 512 - jax.random.randint(jax.random.fold_in(_rk, 8), (4,), 0, max(1, 512 // 4) + 1, jnp.int32)
        _ctx_2048P = jax.random.normal(jax.random.fold_in(_rk, 11), (4, 16, 512), jnp.float32)
        _ctx_2048c = jax.random.dirichlet(jax.random.fold_in(_rk, 511), 0.3 * jnp.ones((16,), jnp.float32), (4, 512))
        _ctx_2048t = jnp.einsum('bsk,bkd->bsd', _ctx_2048c, _ctx_2048P)
        _ctx_2048t = _ctx_2048t * jax.lax.rsqrt(jnp.mean(jnp.square(_ctx_2048t)) + 1e-12) * 0.953939
        ctx_2048 = 2.81802e-05 + 1.00001 * (_ctx_2048t + 0.3 * jax.random.normal(jax.random.fold_in(_rk, 611), (4, 512, 512), jnp.float32))
        _validS = jnp.arange(512)[None, :] < _lenS[:, None]
        _validS2 = jnp.arange(512)[None, :] < _lenS2[:, None]
        _causal = jnp.tril(jnp.ones((512, 512), dtype=bool))
        mask_BxS2_bf1 = jnp.ones((4, 512), dtype=bool)
        mask_Bx1xSxS2_ff0 = jnp.where(jnp.ones((4, 1, 512, 512), dtype=bool), 0.0, -1000000000.0).astype(jnp.float32)
        mask_BxS2_ik0 = jnp.where(jnp.broadcast_to(_validS2[:, :], (4, 512)), 0, 1).astype(jnp.int32)
        return (x, ctx_2048, mask_BxS2_bf1, mask_Bx1xSxS2_ff0, mask_BxS2_ik0)
    x, ctx_2048, mask_BxS2_bf1, mask_Bx1xSxS2_ff0, mask_BxS2_ik0 = _rec_inputs()

    def _L0_xattn_setup():
        import jax, jax.numpy as jnp
        import numpy as np
        D = 512
        H = 16
        HD = D // H
        INNER = 4 * D
        EPS = 1e-05

        def layer_norm(x, w, b):
            mu = jnp.mean(x, axis=-1, keepdims=True)
            var = jnp.mean(jnp.square(x - mu), axis=-1, keepdims=True)
            return (x - mu) * jax.lax.rsqrt(var + EPS) * w + b
        key = jax.random.key(seed)
        ks = jax.random.split(key, 12)
        B, LQ, LK = (4, 256, 512)
        std = 0.02
        inp = {'hidden_states': jax.random.normal(ks[0], (B, LQ, D), jnp.float32), 'encoder_hidden_states': jax.random.normal(ks[1], (B, LK, D), jnp.float32), 'encoder_attention_mask': jnp.ones((B, LK), dtype=bool), 'ln1_w': jnp.ones((D,), jnp.float32), 'ln1_b': jnp.zeros((D,), jnp.float32), 'q_w': jax.random.normal(ks[2], (D, D), jnp.float32) * std, 'q_b': jnp.zeros((D,), jnp.float32), 'k_w': jax.random.normal(ks[3], (D, D), jnp.float32) * std, 'k_b': jnp.zeros((D,), jnp.float32), 'v_w': jax.random.normal(ks[4], (D, D), jnp.float32) * std, 'v_b': jnp.zeros((D,), jnp.float32), 'cproj_w': jax.random.normal(ks[5], (D, D), jnp.float32) * std, 'cproj_b': jnp.zeros((D,), jnp.float32), 'ln2_w': jnp.ones((D,), jnp.float32), 'ln2_b': jnp.zeros((D,), jnp.float32), 'fc_w': jax.random.normal(ks[6], (D, INNER), jnp.float32) * std, 'fc_b': jnp.zeros((INNER,), jnp.float32), 'proj_w': jax.random.normal(ks[7], (INNER, D), jnp.float32) * std, 'proj_b': jnp.zeros((D,), jnp.float32)}
        return inp
    _L0_xattn_all = _L0_xattn_setup()
    _L0_xattn_in = {k: v for k, v in _L0_xattn_all.items() if k in ('ln1_w', 'ln1_b', 'q_w', 'q_b', 'k_w', 'k_b', 'v_w', 'v_b', 'cproj_w', 'cproj_b', 'ln2_w', 'ln2_b', 'fc_w', 'fc_b', 'proj_w', 'proj_b')}
    del _L0_xattn_all

    def _L1_xattn_setup():
        import jax, jax.numpy as jnp
        import numpy as np
        H = 512
        NH = 32
        KVH = 8
        HD = H // NH
        GROUPS = NH // KVH
        EPS = 1e-06
        B, L, S = (4, 256, 256)

        def _gqa_forward(hidden_state, encoder_hidden_state, encoder_attention_mask, Wq, bq, Wk, bk, Wv, bv, Wo, bo, gamma, beta):
            b, l, _ = hidden_state.shape
            s = encoder_hidden_state.shape[1]
            q = hidden_state @ Wq + bq
            k = encoder_hidden_state @ Wk + bk
            v = encoder_hidden_state @ Wv + bv
            q = q.reshape(b, l, KVH, GROUPS, HD).transpose(0, 2, 3, 1, 4)
            k = k.reshape(b, s, KVH, HD).transpose(0, 2, 1, 3)
            v = v.reshape(b, s, KVH, HD).transpose(0, 2, 1, 3)
            scale = 1.0 / jnp.sqrt(jnp.asarray(HD, q.dtype))
            scores = jnp.einsum('bkgld,bksd->bkgls', q, k) * scale
            scores = scores + encoder_attention_mask[:, :, None, :, :]
            attn = jax.nn.softmax(scores, axis=-1)
            out = jnp.einsum('bkgls,bksd->bkgld', attn, v)
            out = out.transpose(0, 3, 1, 2, 4).reshape(b, l, H)
            out = out @ Wo + bo
            x = out + hidden_state
            mu = jnp.mean(x, axis=-1, keepdims=True)
            var = jnp.var(x, axis=-1, keepdims=True)
            return (x - mu) * jax.lax.rsqrt(var + EPS) * gamma + beta
        key = jax.random.key(seed)
        ks = jax.random.split(key, 12)
        sd = 0.02
        return {'hidden_state': jax.random.normal(ks[0], (B, L, H), jnp.float32), 'encoder_hidden_state': jax.random.normal(ks[1], (B, S, H), jnp.float32), 'encoder_attention_mask': jnp.zeros((B, 1, L, S), jnp.float32), 'Wq': jax.random.normal(ks[2], (H, H), jnp.float32) * sd, 'bq': jnp.zeros((H,), jnp.float32), 'Wk': jax.random.normal(ks[3], (H, KVH * HD), jnp.float32) * sd, 'bk': jnp.zeros((KVH * HD,), jnp.float32), 'Wv': jax.random.normal(ks[4], (H, KVH * HD), jnp.float32) * sd, 'bv': jnp.zeros((KVH * HD,), jnp.float32), 'Wo': jax.random.normal(ks[5], (H, H), jnp.float32) * sd, 'bo': jnp.zeros((H,), jnp.float32), 'gamma': jnp.ones((H,), jnp.float32), 'beta': jnp.zeros((H,), jnp.float32)}
    _L1_xattn_all = _L1_xattn_setup()
    _L1_xattn_in = {k: v for k, v in _L1_xattn_all.items() if k in ('Wq', 'bq', 'Wk', 'bk', 'Wv', 'bv', 'Wo', 'bo', 'gamma', 'beta')}
    del _L1_xattn_all

    def _L2_xattn_setup():
        import jax, jax.numpy as jnp
        import numpy as np
        HIDDEN = 512
        HEADS = 16
        HEAD_DIM = HIDDEN // HEADS
        LN_EPS = 1e-05
        GATE_INIT = 0.5

        def _layer_norm(x, gamma, beta):
            mu = jnp.mean(x, axis=-1, keepdims=True)
            var = jnp.mean(jnp.square(x - mu), axis=-1, keepdims=True)
            return (x - mu) * jax.lax.rsqrt(var + LN_EPS) * gamma + beta
        key = jax.random.key(seed)
        ks = jax.random.split(key, 8)
        B, T_TEXT, T_AUDIO = (4, 512, 375)
        s = 0.02
        return {'hidden_states': jax.random.normal(ks[0], (B, T_TEXT, HIDDEN), jnp.float32), 'audio_kv': jax.random.normal(ks[1], (B, T_AUDIO, HIDDEN), jnp.float32), 'audio_attention_mask': jnp.ones((B, T_AUDIO), dtype=bool), 'Wq': jax.random.normal(ks[2], (HIDDEN, HIDDEN), jnp.float32) * s, 'Wk': jax.random.normal(ks[3], (HIDDEN, HIDDEN), jnp.float32) * s, 'Wv': jax.random.normal(ks[4], (HIDDEN, HIDDEN), jnp.float32) * s, 'Wo': jax.random.normal(ks[5], (HIDDEN, HIDDEN), jnp.float32) * s, 'ln_gamma': jnp.ones((HIDDEN,), jnp.float32), 'ln_beta': jnp.zeros((HIDDEN,), jnp.float32), 'gate': jnp.array([GATE_INIT], jnp.float32)}
    _L2_xattn_all = _L2_xattn_setup()
    _L2_xattn_in = {k: v for k, v in _L2_xattn_all.items() if k in ('Wq', 'Wk', 'Wv', 'Wo', 'ln_gamma', 'ln_beta', 'gate')}
    del _L2_xattn_all

    def _L3_xattn_setup():
        import jax, jax.numpy as jnp
        import numpy as np
        B, P, K, H, NH = (4, 512, 64, 512, 16)
        DH = H // NH
        EPS = 1e-06

        def rmsnorm(x, w):
            var = jnp.mean(jnp.square(x), axis=-1, keepdims=True)
            return x * jax.lax.rsqrt(var + EPS) * w
        key = jax.random.key(seed)
        ks = jax.random.split(key, 12)
        s = 0.02
        return {'x': jax.random.normal(ks[0], (B, P, H), jnp.float32), 'latents': jax.random.normal(ks[1], (B, K, H), jnp.float32), 'attention_mask': jax.random.randint(ks[2], (B, P), 0, 2, jnp.int32), 'q_w': s * jax.random.normal(ks[3], (H, H), jnp.float32), 'q_b': jnp.zeros((H,), jnp.float32), 'kv_w': s * jax.random.normal(ks[4], (H, 2 * H), jnp.float32), 'kv_b': jnp.zeros((2 * H,), jnp.float32), 'out_w': s * jax.random.normal(ks[5], (H, H), jnp.float32), 'out_b': jnp.zeros((H,), jnp.float32), 'postnorm_w': jnp.ones((H,), jnp.float32), 'mlp_w1': s * jax.random.normal(ks[6], (H, 4 * H), jnp.float32), 'mlp_b1': jnp.zeros((4 * H,), jnp.float32), 'mlp_w2': s * jax.random.normal(ks[7], (4 * H, H), jnp.float32), 'mlp_b2': jnp.zeros((H,), jnp.float32)}
    _L3_xattn_all = _L3_xattn_setup()
    _L3_xattn_in = {k: v for k, v in _L3_xattn_all.items() if k in ('q_w', 'q_b', 'kv_w', 'kv_b', 'out_w', 'out_b', 'postnorm_w', 'mlp_w1', 'mlp_b1', 'mlp_w2', 'mlp_b2')}
    del _L3_xattn_all
    return {'x': x, 'ctx_2048': ctx_2048, 'mask_BxS2_bf1': mask_BxS2_bf1, 'mask_Bx1xSxS2_ff0': mask_Bx1xSxS2_ff0, 'mask_BxS2_ik0': mask_BxS2_ik0, 'L0_xattn_ln1_w': _L0_xattn_in['ln1_w'], 'L0_xattn_ln1_b': _L0_xattn_in['ln1_b'], 'L0_xattn_q_w': _L0_xattn_in['q_w'], 'L0_xattn_q_b': _L0_xattn_in['q_b'], 'L0_xattn_k_w': _L0_xattn_in['k_w'], 'L0_xattn_k_b': _L0_xattn_in['k_b'], 'L0_xattn_v_w': _L0_xattn_in['v_w'], 'L0_xattn_v_b': _L0_xattn_in['v_b'], 'L0_xattn_cproj_w': _L0_xattn_in['cproj_w'], 'L0_xattn_cproj_b': _L0_xattn_in['cproj_b'], 'L0_xattn_ln2_w': _L0_xattn_in['ln2_w'], 'L0_xattn_ln2_b': _L0_xattn_in['ln2_b'], 'L0_xattn_fc_w': _L0_xattn_in['fc_w'], 'L0_xattn_fc_b': _L0_xattn_in['fc_b'], 'L0_xattn_proj_w': _L0_xattn_in['proj_w'], 'L0_xattn_proj_b': _L0_xattn_in['proj_b'], 'L1_xattn_Wq': _L1_xattn_in['Wq'], 'L1_xattn_bq': _L1_xattn_in['bq'], 'L1_xattn_Wk': _L1_xattn_in['Wk'], 'L1_xattn_bk': _L1_xattn_in['bk'], 'L1_xattn_Wv': _L1_xattn_in['Wv'], 'L1_xattn_bv': _L1_xattn_in['bv'], 'L1_xattn_Wo': _L1_xattn_in['Wo'], 'L1_xattn_bo': _L1_xattn_in['bo'], 'L1_xattn_gamma': _L1_xattn_in['gamma'], 'L1_xattn_beta': _L1_xattn_in['beta'], 'L2_xattn_Wq': _L2_xattn_in['Wq'], 'L2_xattn_Wk': _L2_xattn_in['Wk'], 'L2_xattn_Wv': _L2_xattn_in['Wv'], 'L2_xattn_Wo': _L2_xattn_in['Wo'], 'L2_xattn_ln_gamma': _L2_xattn_in['ln_gamma'], 'L2_xattn_ln_beta': _L2_xattn_in['ln_beta'], 'L2_xattn_gate': _L2_xattn_in['gate'], 'L3_xattn_q_w': _L3_xattn_in['q_w'], 'L3_xattn_q_b': _L3_xattn_in['q_b'], 'L3_xattn_kv_w': _L3_xattn_in['kv_w'], 'L3_xattn_kv_b': _L3_xattn_in['kv_b'], 'L3_xattn_out_w': _L3_xattn_in['out_w'], 'L3_xattn_out_b': _L3_xattn_in['out_b'], 'L3_xattn_postnorm_w': _L3_xattn_in['postnorm_w'], 'L3_xattn_mlp_w1': _L3_xattn_in['mlp_w1'], 'L3_xattn_mlp_b1': _L3_xattn_in['mlp_b1'], 'L3_xattn_mlp_w2': _L3_xattn_in['mlp_w2'], 'L3_xattn_mlp_b2': _L3_xattn_in['mlp_b2']}

def reference(x, ctx_2048, mask_BxS2_bf1, mask_Bx1xSxS2_ff0, mask_BxS2_ik0, L0_xattn_ln1_w, L0_xattn_ln1_b, L0_xattn_q_w, L0_xattn_q_b, L0_xattn_k_w, L0_xattn_k_b, L0_xattn_v_w, L0_xattn_v_b, L0_xattn_cproj_w, L0_xattn_cproj_b, L0_xattn_ln2_w, L0_xattn_ln2_b, L0_xattn_fc_w, L0_xattn_fc_b, L0_xattn_proj_w, L0_xattn_proj_b, L1_xattn_Wq, L1_xattn_bq, L1_xattn_Wk, L1_xattn_bk, L1_xattn_Wv, L1_xattn_bv, L1_xattn_Wo, L1_xattn_bo, L1_xattn_gamma, L1_xattn_beta, L2_xattn_Wq, L2_xattn_Wk, L2_xattn_Wv, L2_xattn_Wo, L2_xattn_ln_gamma, L2_xattn_ln_beta, L2_xattn_gate, L3_xattn_q_w, L3_xattn_q_b, L3_xattn_kv_w, L3_xattn_kv_b, L3_xattn_out_w, L3_xattn_out_b, L3_xattn_postnorm_w, L3_xattn_mlp_w1, L3_xattn_mlp_b1, L3_xattn_mlp_w2, L3_xattn_mlp_b2):
    import jax
    import jax.numpy as jnp

    def _L0_xattn_ref(hidden_states, encoder_hidden_states, encoder_attention_mask, ln1_w, ln1_b, q_w, q_b, k_w, k_b, v_w, v_b, cproj_w, cproj_b, ln2_w, ln2_b, fc_w, fc_b, proj_w, proj_b):
        import jax, jax.numpy as jnp
        import numpy as np
        D = 512
        H = 16
        HD = D // H
        INNER = 4 * D
        EPS = 1e-05

        def layer_norm(x, w, b):
            mu = jnp.mean(x, axis=-1, keepdims=True)
            var = jnp.mean(jnp.square(x - mu), axis=-1, keepdims=True)
            return (x - mu) * jax.lax.rsqrt(var + EPS) * w + b
        B, LQ, _ = hidden_states.shape
        LK = encoder_hidden_states.shape[1]
        residual = hidden_states
        x = layer_norm(hidden_states, ln1_w, ln1_b)
        q = (x @ q_w + q_b).reshape(B, LQ, H, HD).transpose(0, 2, 1, 3)
        k = (encoder_hidden_states @ k_w + k_b).reshape(B, LK, H, HD).transpose(0, 2, 1, 3)
        v = (encoder_hidden_states @ v_w + v_b).reshape(B, LK, H, HD).transpose(0, 2, 1, 3)
        scale = 1.0 / np.sqrt(HD).astype(np.float32)
        scores = jnp.einsum('bhqd,bhkd->bhqk', q, k) * scale
        mask = encoder_attention_mask[:, None, None, :]
        mask_value = jnp.finfo(scores.dtype).min
        scores = jnp.where(mask, scores, mask_value)
        attn = jax.nn.softmax(scores, axis=-1)
        out = jnp.einsum('bhqk,bhkd->bhqd', attn, v)
        out = out.transpose(0, 2, 1, 3).reshape(B, LQ, D)
        out = out @ cproj_w + cproj_b
        hidden = out + residual
        residual = hidden
        y = layer_norm(hidden, ln2_w, ln2_b)
        y = jax.nn.gelu(y @ fc_w + fc_b, approximate=True)
        y = y @ proj_w + proj_b
        return residual + y

    def _L1_xattn_ref(hidden_state, encoder_hidden_state, encoder_attention_mask, Wq, bq, Wk, bk, Wv, bv, Wo, bo, gamma, beta):
        import jax, jax.numpy as jnp
        import numpy as np
        H = 512
        NH = 32
        KVH = 8
        HD = H // NH
        GROUPS = NH // KVH
        EPS = 1e-06
        B, L, S = (4, 256, 256)

        def _gqa_forward(hidden_state, encoder_hidden_state, encoder_attention_mask, Wq, bq, Wk, bk, Wv, bv, Wo, bo, gamma, beta):
            b, l, _ = hidden_state.shape
            s = encoder_hidden_state.shape[1]
            q = hidden_state @ Wq + bq
            k = encoder_hidden_state @ Wk + bk
            v = encoder_hidden_state @ Wv + bv
            q = q.reshape(b, l, KVH, GROUPS, HD).transpose(0, 2, 3, 1, 4)
            k = k.reshape(b, s, KVH, HD).transpose(0, 2, 1, 3)
            v = v.reshape(b, s, KVH, HD).transpose(0, 2, 1, 3)
            scale = 1.0 / jnp.sqrt(jnp.asarray(HD, q.dtype))
            scores = jnp.einsum('bkgld,bksd->bkgls', q, k) * scale
            scores = scores + encoder_attention_mask[:, :, None, :, :]
            attn = jax.nn.softmax(scores, axis=-1)
            out = jnp.einsum('bkgls,bksd->bkgld', attn, v)
            out = out.transpose(0, 3, 1, 2, 4).reshape(b, l, H)
            out = out @ Wo + bo
            x = out + hidden_state
            mu = jnp.mean(x, axis=-1, keepdims=True)
            var = jnp.var(x, axis=-1, keepdims=True)
            return (x - mu) * jax.lax.rsqrt(var + EPS) * gamma + beta
        return _gqa_forward(hidden_state, encoder_hidden_state, encoder_attention_mask, Wq, bq, Wk, bk, Wv, bv, Wo, bo, gamma, beta)

    def _L2_xattn_ref(hidden_states, audio_kv, audio_attention_mask, Wq, Wk, Wv, Wo, ln_gamma, ln_beta, gate):
        import jax, jax.numpy as jnp
        import numpy as np
        HIDDEN = 512
        HEADS = 16
        HEAD_DIM = HIDDEN // HEADS
        LN_EPS = 1e-05
        GATE_INIT = 0.5

        def _layer_norm(x, gamma, beta):
            mu = jnp.mean(x, axis=-1, keepdims=True)
            var = jnp.mean(jnp.square(x - mu), axis=-1, keepdims=True)
            return (x - mu) * jax.lax.rsqrt(var + LN_EPS) * gamma + beta
        B, Tt, D = hidden_states.shape
        Ta = audio_kv.shape[1]
        scale = HEAD_DIM ** (-0.5)
        a = _layer_norm(audio_kv, ln_gamma, ln_beta)
        Q = (hidden_states @ Wq.T).reshape(B, Tt, HEADS, HEAD_DIM).transpose(0, 2, 1, 3)
        K = (a @ Wk.T).reshape(B, Ta, HEADS, HEAD_DIM).transpose(0, 2, 1, 3)
        V = (a @ Wv.T).reshape(B, Ta, HEADS, HEAD_DIM).transpose(0, 2, 1, 3)
        scores = jnp.einsum('bhtd,bhsd->bhts', Q, K) * scale
        mask = audio_attention_mask[:, None, None, :]
        scores = jnp.where(mask, scores, jnp.float32(-jnp.inf))
        attn = jax.nn.softmax(scores, axis=-1)
        out = jnp.einsum('bhts,bhsd->bhtd', attn, V)
        out = out.transpose(0, 2, 1, 3).reshape(B, Tt, D)
        out = out @ Wo.T
        return hidden_states + jnp.tanh(gate) * out

    def _L3_xattn_ref(x, latents, attention_mask, q_w, q_b, kv_w, kv_b, out_w, out_b, postnorm_w, mlp_w1, mlp_b1, mlp_w2, mlp_b2):
        import jax, jax.numpy as jnp
        import numpy as np
        B, P, K, H, NH = (4, 512, 64, 512, 16)
        DH = H // NH
        EPS = 1e-06

        def rmsnorm(x, w):
            var = jnp.mean(jnp.square(x), axis=-1, keepdims=True)
            return x * jax.lax.rsqrt(var + EPS) * w
        b, p, _ = x.shape
        k_len = latents.shape[1]
        residual = latents
        h = jnp.concatenate([x, latents], axis=1)
        q = (latents @ q_w + q_b).reshape(b, k_len, NH, DH)
        kv = (h @ kv_w + kv_b).reshape(b, p + k_len, NH, DH, 2)
        kmat, v = (kv[..., 0], kv[..., 1])
        attn = jnp.einsum('bkhd,bnhd->bhkn', q, kmat) / DH
        full_mask = jnp.concatenate([attention_mask.astype(bool), jnp.ones((b, k_len), bool)], axis=-1)
        attn = jnp.where(full_mask[:, None, None, :], attn, -jnp.inf)
        attn = jax.nn.softmax(attn.astype(jnp.float32), axis=-1).astype(q.dtype)
        attn_out = jnp.einsum('bhkn,bnhd->bkhd', attn, v).reshape(b, k_len, H)
        attn_out = attn_out @ out_w + out_b + residual
        out = rmsnorm(attn_out, postnorm_w)
        out = jax.nn.gelu(out @ mlp_w1 + mlp_b1) @ mlp_w2 + mlp_b2
        return out + residual
    x = _L0_xattn_ref(x, ctx_2048, mask_BxS2_bf1, L0_xattn_ln1_w, L0_xattn_ln1_b, L0_xattn_q_w, L0_xattn_q_b, L0_xattn_k_w, L0_xattn_k_b, L0_xattn_v_w, L0_xattn_v_b, L0_xattn_cproj_w, L0_xattn_cproj_b, L0_xattn_ln2_w, L0_xattn_ln2_b, L0_xattn_fc_w, L0_xattn_fc_b, L0_xattn_proj_w, L0_xattn_proj_b)
    x = _L1_xattn_ref(x, ctx_2048, mask_Bx1xSxS2_ff0, L1_xattn_Wq, L1_xattn_bq, L1_xattn_Wk, L1_xattn_bk, L1_xattn_Wv, L1_xattn_bv, L1_xattn_Wo, L1_xattn_bo, L1_xattn_gamma, L1_xattn_beta)
    x = _L2_xattn_ref(x, ctx_2048, mask_BxS2_bf1, L2_xattn_Wq, L2_xattn_Wk, L2_xattn_Wv, L2_xattn_Wo, L2_xattn_ln_gamma, L2_xattn_ln_beta, L2_xattn_gate)
    x = _L3_xattn_ref(ctx_2048, x, mask_BxS2_ik0, L3_xattn_q_w, L3_xattn_q_b, L3_xattn_kv_w, L3_xattn_kv_b, L3_xattn_out_w, L3_xattn_out_b, L3_xattn_postnorm_w, L3_xattn_mlp_w1, L3_xattn_mlp_b1, L3_xattn_mlp_w2, L3_xattn_mlp_b2)
    return x

_drawn_inputs = setup_inputs


def setup_inputs(seed=0):
    import zlib

    import numpy as np

    out = dict(_drawn_inputs(seed))
    spreads = {'L0_xattn_ln1_w': (1.0, 0.6),
     'L0_xattn_ln1_b': (0.0, 0.8),
     'L0_xattn_q_b': (0.0, 0.8),
     'L0_xattn_k_b': (0.0, 2.0),
     'L0_xattn_v_b': (0.0, 0.1),
     'L0_xattn_cproj_b': (0.0, 0.1),
     'L0_xattn_ln2_w': (1.0, 0.2),
     'L0_xattn_ln2_b': (0.0, 0.362),
     'L0_xattn_fc_b': (0.0, 0.1),
     'L0_xattn_proj_b': (0.0, 0.1),
     'L1_xattn_bq': (0.0, 0.8),
     'L1_xattn_bk': (0.0, 2.0),
     'L1_xattn_bv': (0.0, 0.1),
     'L1_xattn_bo': (0.0, 0.1),
     'L1_xattn_gamma': (1.0, 0.2),
     'L1_xattn_beta': (0.0, 0.1),
     'L2_xattn_ln_gamma': (1.0, 0.6),
     'L2_xattn_ln_beta': (0.0, 0.8),
     'L3_xattn_q_b': (0.0, 2.0),
     'L3_xattn_kv_b': (0.0, 0.8),
     'L3_xattn_out_b': (0.0, 0.374),
     'L3_xattn_postnorm_w': (1.0, 0.2),
     'L3_xattn_mlp_b1': (0.0, 0.1),
     'L3_xattn_mlp_b2': (0.0, 0.1)}
    factors = {'L0_xattn_q_w': 7.513,
     'L0_xattn_k_w': 7.446,
     'L1_xattn_Wq': 8.0,
     'L1_xattn_Wk': 8.0,
     'L2_xattn_Wq': 8.0,
     'L2_xattn_Wk': 8.0,
     'L3_xattn_q_w': 8.0,
     'L3_xattn_kv_w': 5.198,
     'L3_xattn_out_w': 3.83}
    for name, (base, spread) in spreads.items():
        noise = np.random.default_rng([zlib.crc32(name.encode()), seed]).standard_normal(out[name].shape)
        drawn = base * np.exp(spread * noise) if base else spread * noise
        out[name] = jnp.asarray(drawn.astype(out[name].dtype))
    for name, factor in factors.items():
        out[name] = (out[name] * factor).astype(out[name].dtype)
    return out
```

```python
from contextlib import ExitStack

import numpy as np

import concourse.bass as bass
from concourse import mybir

ALU = mybir.AluOpType
ACT = mybir.ActivationFunctionType
AX = mybir.AxisListType
F32 = mybir.dt.float32
F32R = mybir.dt.float32r
U8 = mybir.dt.uint8
I32 = mybir.dt.int32

P = 128
B, S, D = 4, 512, 512
NT = S // P
NC = D // P
NFB = 4
MASKED = -(2.0 ** 100)
LOWEST = float(np.finfo(np.float32).min)
WSLOTS = 4
PTB = 3
RING = 2


class Layer:
    def __init__(self, n, hd, units, keys, scale, eps, vcols):
        self.n, self.hd, self.units, self.keys, self.scale, self.eps = n, hd, units, keys, scale, eps
        self.copies = 3 if hd == 32 else 4
        self.row = self.copies * hd
        self.kt = keys // P
        self.halves = keys // S
        self.slots = 4 * self.kt // 2
        self.kheads = 4 if hd == 32 else 1
        self.vcols = vcols


LAYERS = [
    Layer(0, 32, 4, 512, 32 ** -0.5, 1e-5, 512),
    Layer(1, 16, 8, 512, 1.0, 1e-6, 128),
    Layer(2, 32, 4, 512, 32 ** -0.5, 1e-5, 512),
    Layer(3, 32, 4, 1024, 1.0 / 32, 1e-6, 512),
]
UNITS = [(L.n, u) for L in LAYERS for u in range(L.units)]

WEIGHTS = []
for _n in range(4):
    WEIGHTS += [(_n, w) for w in (("v", "k", "q", "o") if _n == 1 else ("v", "q", "k", "o"))]
    if _n in (0, 3):
        WEIGHTS += [(_n, f"{w}{f}") for f in range(NFB) for w in ("up", "down")]
WINDEX = {w: i for i, w in enumerate(WEIGHTS)}


def layer_steps(L):
    n = L.n

    def project(u):
        out = []
        if n != 1 or u % 2 == 0:
            out.append(("q", n, u if n != 1 else u // 2))
        if n != 1 or u == 0:
            out += [("k", n, u, h) for h in range(L.halves)]
        return out + [("stack", n, u)]

    def maxima(u):
        return [("max", n, u, j, t, h) for j in range(4) for t in range(NT) for h in range(L.halves)] + [("maxT", n, u)]

    steps = []
    if n == 0:
        steps += [("ctxT", c) for c in range(NC)]
        steps += [("norm", 0, "x")] + [("xT", 0, "z", c) for c in range(NC)]
    elif n == 1:
        steps += [("mask_in",)] + [("xT", 1, "x", c) for c in range(NC)] + [("maskT", t) for t in range(NT)]
    elif n == 2:
        steps += [("norm", 2, "ctx")] + [("aT", c) for c in range(NC)] + [("xT", 2, "x", c) for c in range(NC)]
    else:
        steps += [("xT", 3, "x", c) for c in range(NC)]
    steps += [("v", n, t) for t in range(L.kt)]
    steps += project(0) + project(1) + maxima(0)
    for u in range(L.units):
        fill = (maxima(u + 1) if u + 1 < L.units else [])
        late = (project(u + 2) if u + 2 < L.units else [])
        stack = [s for s in late if s[0] == "stack"]
        fill += [s for s in late if s[0] != "stack"]
        done = 0
        steps.append(("score", n, u, 0))
        for s in range(L.slots):
            if s + 1 < L.slots:
                steps.append(("score", n, u, s + 1))
            upto = len(fill) * (s + 1) // L.slots
            steps += fill[done:upto]
            done = upto
            steps.append(("pv", n, u, s))
        steps += [("heads", n, u)] + stack
    steps += [("o", n, t) for t in range(NT)]
    if n in (0, 3):
        steps += [("norm", n, "mid")] + [("xT", n, "mid", c) for c in range(NC)]
        for f in range(NFB):
            steps += [("up", n, f, m) for m in range(NC)]
            if f:
                steps.append(("down", n, f - 1))
        steps += [("down", n, NFB - 1), ("mlp_out", n)]
    elif n == 1:
        steps += [("norm", 1, "out")]
    return steps


STEPS = [s for L in LAYERS for s in layer_steps(L)]
RINGED = ("ctxT", "xT", "aT", "maskT", "v", "q", "k", "max", "maxT", "o", "up")
RING_STEPS = [s for s in STEPS if s[0] in RINGED]
RINDEX = {s: i for i, s in enumerate(RING_STEPS)}
SCORE_STEPS = [s for s in STEPS if s[0] == "score"]
SINDEX = {s: i for i, s in enumerate(SCORE_STEPS)}


def last_use():
    out = {}
    for i, (n, name) in enumerate(WEIGHTS):
        if name[:2] == "up":
            out["up", n, int(name[2:]), NC - 1] = i
        elif name[:4] == "down":
            out["down", n, int(name[4:])] = i
        else:
            out[[s for s in STEPS if s[:2] == (name, n)][-1]] = i
    return out


LAST_USE = last_use()


def order(kinds):
    return {s: i + 1 for i, s in enumerate([s for s in STEPS if s[0] in kinds])}


def build(nc, A, out):
    ctx = ExitStack()

    def sb(name, shape, dt=F32):
        return ctx.enter_context(nc.sbuf_tensor(name, shape, dt))

    def sem(name):
        s = ctx.enter_context(nc.semaphore(name))
        sems.append(s)
        return s

    with ctx:
        sems = []
        w = sb("w", [P, WSLOTS, NC, D])
        x = sb("x", [P, NT, D])
        ctxT = sb("ctxT", [P, NC, S])
        xT = sb("xT", [P, NC, S])
        at = sb("at", [P, NC, S])
        v = sb("v", [P, 8, D])
        cx = v[:, 0:NT, :]
        wide = sb("wide", [P, 2, NC, D])
        qs = sb("qs", [P, 2, 4, S], F32R)
        ks = sb("ks", [P, 2, 4, 2 * S], F32R)
        q_hi = sb("q_hi", [P, S], F32R)
        q_lo = sb("q_lo", [P, S], F32R)
        k_hi = sb("k_hi", [P, 2 * S], F32R)
        k_lo = sb("k_lo", [P, 2 * S], F32R)
        q_full = sb("q_full", [P, S])
        pt = sb("pt", [P, PTB, 2, S])
        heads1 = sb("heads1", [P, S])
        rden = sb("rden", [P, S])
        vone = sb("vone", [P, NT, 8, 32])
        mcol = sb("mcol", [P, 2, 2, 16])
        nm_hi = sb("nm_hi", [16, P], F32R)
        nm_lo = sb("nm_lo", [16, P], F32R)
        krow = sb("krow", [3, 3, S], F32R)
        m8 = sb("m8", [1, S], U8)
        m32 = rden[0:1, :].bitcast(I32)
        mtmp = q_full[0:1, :]
        mcolk = sb("mcolk", [P, NT])
        m8c = sb("m8c", [P, NT], U8)
        ones = sb("ones", [P, 32])
        ident = sb("ident", [P, P])
        stats = sb("stats", [P, NT, 6])
        mv = sb("mv", [P, NT, 2])
        rstd = sb("rstd", [P, NT])
        var = sb("var", [P, NT])
        minus_half = sb("minus_half", [P, NT])
        gate = sb("gate", [P, 1])
        gtanh = sb("gtanh", [P, 1])
        bias = {k: sb(f"c_{k}", [P, NC]) for k in
                ("q0", "k0", "q1", "q3", "k3", "w10", "b10", "w20", "b20", "w2", "b2", "w3")}
        bias["k1"] = sb("c_k1", [P, 1])
        bq4 = sb("bq4", [P, NC])
        bup = {0: sb("c_up0", [P, NFB * NC]), 3: sb("c_up3", [P, NFB * NC])}
        row = {k: sb(f"r_{k}", [P, D]) for k in
               ("v0", "o0", "down0", "o1", "gamma1", "beta1", "v3", "o3", "down3")}
        row["v1"] = sb("r_v1", [P, 128])

        banks = [ctx.enter_context(nc.psum_tensor(f"bank{i}", [P, 512], F32)) for i in range(4, 8)]
        score_banks = ctx.enter_context(nc.psum_tensor("score_banks", [P, 4, 512], F32))
        ring = banks[0:2]
        num, den = banks[2], banks[3]

        const_in = ctx.enter_context(nc.semaphore("const_in"))
        const_set = ctx.enter_context(nc.semaphore("const_set"))
        gate_set = ctx.enter_context(nc.semaphore("gate_set"))
        x_in, ctx_in, mask_in, out_stored = sem("x_in"), sem("ctx_in"), sem("mask_in"), sem("out_stored")
        keymask_in = sem("keymask_in")
        keymask_set = sem("keymask_set")
        w_in = [sem(f"w_in{i}") for i in range(WSLOTS)]
        ring_full = sem("ring_full")
        ring_free = [sem(f"ring_free{i}") for i in range(RING)]
        by_vector = sem("by_vector")
        by_scalar = sem("by_scalar")
        norm_done = sem("norm_done")
        var_done, rstd_done = sem("var_done"), sem("rstd_done")
        hi_done = sem("hi_done")
        stacked = [sem(f"stacked{i}") for i in range(2)]
        max_done = sem("max_done")
        mrow_in = sem("mrow_in")
        score_full, score_masked = sem("score_full"), sem("score_masked")
        exp_done, pv_done = sem("exp_done"), sem("pv_done")
        heads_done = sem("heads_done")
        heads1_moved = sem("heads1_moved")
        at1_done = sem("at1_done")
        down_done = sem("down_done")
        mlp_done = sem("mlp_done")

        N_NORM = order(("norm",))
        N_QK = order(("q", "k"))
        N_MAXT, N_SCORE, N_PV = order(("maxT",)), order(("score",)), order(("pv",))
        N_HEADS = order(("heads",))
        N_DOWN, N_MLP = order(("down",)), order(("mlp_out",))
        N_SCORE1 = {s: i + 1 for i, s in enumerate([s for s in SCORE_STEPS if s[1] == 1])}

        def unit_at(n, u):
            return UNITS.index((n, u))

        STACK_DMAS = [(4 + LAYERS[n].kheads) * LAYERS[n].copies + 1 + LAYERS[n].halves for n, _ in UNITS]

        def stack_value(g):
            return 16 * sum(STACK_DMAS[i] for i in range(g % 2, g + 1, 2))

        def last_pv(g):
            n, u = UNITS[g]
            return N_PV[("pv", n, u, LAYERS[n].slots - 1)]

        def last_project(n, u):
            if n == 1:
                return max(("q", 1, u // 2), ("k", 1, 0, 0), key=RINDEX.get)
            return ("k", n, u, LAYERS[n].halves - 1)

        def ring_bank(step):
            return ring[RINDEX[step] % RING]

        def wait_ring_full(eng, step):
            eng.wait_ge(ring_full, RINDEX[step] + 1)

        def free_of(step):
            return ring_free[RINDEX[step] % RING]

        def wait_moved(eng, step):
            for i in range(max(RINDEX[step] - RING + 1, 0), RINDEX[step] + 1):
                eng.wait_ge(ring_free[i % RING], i // RING + 1)

        def wait_weights_used(eng, n, name):
            step = [s for s, i in LAST_USE.items() if WEIGHTS[i] == (n, name)][0]
            if step[0] == "down":
                eng.wait_ge(down_done, N_DOWN[step])
            else:
                wait_ring_full(eng, step)

        def w_ap(n, name):
            return w[:, WINDEX[(n, name)] % WSLOTS]

        def bcast(ap, cols):
            return ap.rearrange("(o n) -> o n", o=1).broadcast_to([P, cols])

        zrow = at

        CONSTS = []
        for key, name in (("q0", "L0_xattn_q_b"), ("k0", "L0_xattn_k_b"), ("q1", "L1_xattn_bq"), ("k1", "L1_xattn_bk"),
                          ("q3", "L3_xattn_q_b"), ("k3", "L3_k_b"), ("w10", "L0_xattn_ln1_w"),
                          ("b10", "L0_xattn_ln1_b"), ("w20", "L0_xattn_ln2_w"), ("b20", "L0_xattn_ln2_b"),
                          ("w2", "L2_xattn_ln_gamma"), ("b2", "L2_xattn_ln_beta"), ("w3", "L3_xattn_postnorm_w")):
            CONSTS.append((bias[key][:, :], A[name]))
        CONSTS.append((bup[0][:, :], A["L0_xattn_fc_b"]))
        CONSTS.append((bup[3][:, :], A["L3_xattn_mlp_b1"]))
        for key, name in (("v0", "L0_xattn_v_b"), ("o0", "L0_xattn_cproj_b"), ("down0", "L0_xattn_proj_b"),
                          ("v1", "L1_xattn_bv"), ("o1", "L1_xattn_bo"), ("gamma1", "L1_xattn_gamma"),
                          ("beta1", "L1_xattn_beta"), ("v3", "L3_v_b"), ("o3", "L3_xattn_out_b"),
                          ("down3", "L3_xattn_mlp_b2")):
            CONSTS.append((row[key][:, :], bcast(A[name], row[key].shape[1])))
        CONSTS.append((gate[:, :], bcast(A["L2_xattn_gate"], 1)))

        with nc.Block() as block:
            @block.sync
            def _(sp):
                for dst, src in CONSTS:
                    sp.dma_start(dst, src, allow_slow_non_contiguous=True).then_inc(const_in, 16)

            @block.gpsimd
            def _(pool):
                nc.gpsimd.memset(ident[:, :], 0.0).then_inc(const_set, 1)
                nc.gpsimd.memset(ones[:, :], 1.0).then_inc(const_set, 1)
                nc.gpsimd.memset(krow[:, :, :].bitcast(F32), 1.0).then_inc(const_set, 1)
                nc.gpsimd.memset(vone[:, :, :, :], 1.0).then_inc(const_set, 1)
                nc.gpsimd.memset(minus_half[:, :], -0.5).then_inc(const_set, 1)
                pool.wait_ge(const_set, 5)
                nc.gpsimd.affine_select(out=ident[:, :], in_=ident[:, :], compare_op=ALU.not_equal, fill=1.0,
                                        base=0, pattern=[[-1, P]], channel_multiplier=1).then_inc(const_set, 1)
                nc.gpsimd.memset(krow[0:1, 2:3, :].bitcast(F32), 0.0).then_inc(const_set, 1)

            @block.scalar
            def _(act):
                act.wait_ge(const_in, 16 * len(CONSTS))
                nc.scalar.activation(gtanh[:, :], gate[:, :], ACT.Tanh).then_inc(gate_set, 1)
                nc.scalar.activation(bq4[:, :], bias["q1"][:, :], ACT.Copy, scale=0.25).then_inc(gate_set, 1)

            @block.vector
            def _(dve):
                dve.wait_ge(const_in, 16 * len(CONSTS))
                dve.wait_ge(const_set, 7)
                dve.wait_ge(gate_set, 2)

        with nc.Fori(0, B) as b:
            block = nc.Block()
            with block:
                @block.sync
                def _(sp):
                    def tokens(ap):
                        return ap[bass.ds(b, 1)].rearrange("o (t p) d -> p (o t) d", p=P)

                    def load_weights(i):
                        n, name = WEIGHTS[i]
                        if i >= WSLOTS:
                            wait_weights_used(sp, *WEIGHTS[i - WSLOTS])
                        if name[:2] == "up":
                            f = int(name[2:])
                            src = A[f"up{n}"][:, f * D:(f + 1) * D]
                        elif name[:4] == "down":
                            f = int(name[4:])
                            src = A[f"down{n}"][f * D:(f + 1) * D, :]
                        else:
                            src = A[f"{name}{n}"]
                        sp.dma_start(w[:, i % WSLOTS, :, 0:src.shape[1]], src.rearrange("(c p) n -> p c n", p=P)
                                       ).then_inc(w_in[i % WSLOTS], 16)

                    sp.dma_start(cx, tokens(A["ctx_2048"])).then_inc(ctx_in, 16)
                    sp.dma_start(x[:, :, :], tokens(A["x"])).then_inc(x_in, 16)
                    sp.dma_start(m8[:, :], A["mask8"][bass.ds(b, 1), :]).then_inc(keymask_in, 16)
                    sp.dma_start(m32, A["mask_BxS2_ik0"][bass.ds(b, 1), :]).then_inc(keymask_in, 16)
                    sp.dma_start(m8c[:, :], A["mask8_cols"][bass.ds(b, 1)].rearrange("o p t -> p (o t)")
                                 ).then_inc(keymask_in, 16)
                    for i in range(WSLOTS):
                        load_weights(i)
                    sp.wait_ge(keymask_set, 1)
                    for step in STEPS:
                        kind, n = step[0], step[1] if len(step) > 1 else None
                        if kind == "mask_in":
                            sp.wait_ge(pv_done, last_pv(unit_at(0, 3)))
                            sp.dma_start(cx, tokens(A["ctx_2048"])).then_inc(ctx_in, 16)
                            sp.wait_ge(mlp_done, N_MLP[("mlp_out", 0)])
                            sp.dma_start(wide[:, 0], A["mask_Bx1xSxS2_ff0"][bass.ds(b, 1)].rearrange(
                                "o a (t p) k -> p (o a t) k", p=P)).then_inc(mask_in, 16)
                        elif kind == "stack":
                            u, L = step[2], LAYERS[n]
                            g, hd, cp = unit_at(n, u), L.hd, L.copies
                            wait_moved(sp, last_project(n, u))
                            if g >= 2:
                                sp.wait_ge(pv_done, last_pv(g - 2))
                            q0 = 0 if hd == 32 else 64 * (u % 2)
                            for i in range(cp):
                                part = (q_hi, q_lo)[i % 2]
                                for j in range(4):
                                    sp.dma_start(qs[hd * i:hd * (i + 1), g % 2, j].bitcast(F32),
                                                 part[q0 + j * hd:q0 + (j + 1) * hd, :].bitcast(F32)
                                                 ).then_inc(stacked[g % 2], 16)
                            sp.dma_start(qs[L.row:L.row + 1, g % 2].bitcast(F32),
                                         krow[1:2, 0:1, :].bitcast(F32).broadcast_to([1, 4, S])
                                         ).then_inc(stacked[g % 2], 16)
                            k0 = 0 if hd == 32 else 16 * u
                            for i in range(cp):
                                part = (k_hi, k_hi, k_lo, k_lo)[i]
                                for j in range(L.kheads):
                                    sp.dma_start(ks[hd * i:hd * (i + 1), g % 2, j, 0:L.keys].bitcast(F32),
                                                 part[k0 + j * hd:k0 + (j + 1) * hd, 0:L.keys].bitcast(F32)
                                                 ).then_inc(stacked[g % 2], 16)
                            for h, which in enumerate(((0,), (2,), (0,), (1, 2))[n]):
                                sp.dma_start(ks[L.row:L.row + 3, g % 2, 0:L.kheads, h * S:(h + 1) * S].bitcast(F32),
                                             krow[:, which:which + 1, :].bitcast(F32).broadcast_to([3, L.kheads, S])
                                             ).then_inc(stacked[g % 2], 16)
                        elif kind == "maxT":
                            u, L = step[2], LAYERS[n]
                            g = unit_at(n, u)
                            wait_moved(sp, step)
                            for i, part in enumerate((nm_hi, nm_lo)):
                                sp.dma_start(qs[L.row + 1 + i:L.row + 2 + i, g % 2].bitcast(F32).rearrange(
                                    "o j (t n) -> o (j t) n", n=P), part[:, :].bitcast(F32)).then_inc(mrow_in, 16)
                        elif kind == "heads" and n == 1:
                            u = step[2]
                            sp.wait_ge(heads_done, N_HEADS[step])
                            if u % 2 == 0 and u >= 2:
                                sp.wait_ge(at1_done, u // 2)
                            r = 64 * (u % 2)
                            for j in range(4):
                                sp.dma_start(at[r + 16 * j:r + 16 * j + 16, u // 2, :],
                                             heads1[32 * j:32 * j + 16, :]).then_inc(heads1_moved, 16)
                                sp.dma_start(rden[r + 16 * j:r + 16 * j + 16, :],
                                             heads1[32 * j + 16:32 * j + 32, :]).then_inc(heads1_moved, 16)
                        if step in LAST_USE and LAST_USE[step] + WSLOTS < len(WEIGHTS):
                            load_weights(LAST_USE[step] + WSLOTS)
                    sp.wait_ge(mlp_done, N_MLP[("mlp_out", 3)])
                    sp.dma_start(out[bass.ds(b, 1)].rearrange("o (t p) d -> p (o t) d", p=P), x[:, :, :]
                                 ).then_inc(out_stored, 16)
                    sp.wait_ge(out_stored, 16)

                @block.gpsimd
                def _(pool):
                    for step in STEPS:
                        if step[0] == "norm":
                            pool.wait_ge(var_done, N_NORM[step])
                            nc.gpsimd.tensor_tensor(rstd[:, :], var[:, :], minus_half[:, :], ALU.pow
                                                    ).then_inc(rstd_done, 1)

                @block.tensor
                def _(pe):
                    landed = [0]

                    def need_weight(n, name):
                        i = WINDEX[(n, name)]
                        while landed[0] <= i:
                            k = landed[0]
                            pe.wait_ge(w_in[k % WSLOTS], 16 * (k // WSLOTS + 1))
                            landed[0] += 1

                    def take_ring(step):
                        i = RINDEX[step]
                        if i >= RING:
                            pe.wait_ge(ring_free[i % RING], i // RING)
                        return ring[i % RING]

                    def project_T(step, n, name, cols, src, c0=0):
                        o = take_ring(step)
                        wt = w_ap(n, name)
                        for c in range(NC):
                            last = nc.tensor.matmul(o[:, :], wt[:, c, cols[0]:cols[1]], src[:, c, :],
                                                    start=(c == 0), stop=(c == NC - 1))
                        return last

                    for step in STEPS:
                        kind, n = step[0], step[1] if len(step) > 1 else None
                        L = LAYERS[n] if n in (0, 1, 2, 3) else None
                        if kind in ("ctxT", "xT", "aT", "maskT"):
                            if kind == "ctxT":
                                pe.wait_ge(ctx_in, 16)
                                src, c = cx, step[1]
                            elif kind == "xT":
                                src, c = {"x": x, "z": zrow, "mid": zrow}[step[2]], step[3]
                                if step[2] == "z":
                                    pe.wait_ge(norm_done, N_NORM[("norm", 0, "x")])
                                elif step[2] == "mid":
                                    pe.wait_ge(norm_done, N_NORM[("norm", n, "mid")])
                                elif n == 1:
                                    pe.wait_ge(mlp_done, N_MLP[("mlp_out", 0)])
                                elif n == 2:
                                    pe.wait_ge(norm_done, N_NORM[("norm", 1, "out")])
                                else:
                                    wait_moved(pe, ("o", 2, NT - 1))
                            elif kind == "aT":
                                pe.wait_ge(norm_done, N_NORM[("norm", 2, "ctx")])
                                src, c = zrow, step[1]
                            else:
                                pe.wait_ge(mask_in, 16)
                                src, c = wide[:, 0], step[1]
                            o = take_ring(step)
                            for t in range(NT):
                                last = nc.tensor.transpose(o[:, t * P:(t + 1) * P], src[:, t, c * P:(c + 1) * P], ident[:, :])
                            last.then_inc(ring_full, 1)
                        elif kind == "v":
                            t = step[2]
                            need_weight(n, "v")
                            if n == 2:
                                wait_moved(pe, ("aT", NC - 1))
                                src, t0 = wide[:, 0], t
                            elif t < NT:
                                wait_moved(pe, ("ctxT", NC - 1))
                                src, t0 = ctxT, t
                            else:
                                wait_moved(pe, ("xT", 3, "x", NC - 1))
                                src, t0 = xT, t - NT
                            o = take_ring(step)
                            wt = w_ap(n, "v")
                            for c in range(NC):
                                last = nc.tensor.matmul(o[:, 0:L.vcols], src[:, c, t0 * P:(t0 + 1) * P], wt[:, c, 0:L.vcols],
                                                        start=(c == 0), stop=(c == NC - 1))
                            last.then_inc(ring_full, 1)
                        elif kind in ("q", "k"):
                            u = step[2]
                            need_weight(n, kind)
                            if kind == "q":
                                wait_moved(pe, ("xT", n, "z" if n == 0 else "x", NC - 1))
                                src = xT
                            else:
                                if n == 2:
                                    src = wide[:, 0]
                                elif step[3] == 1:
                                    src = xT
                                else:
                                    src = ctxT
                            last = project_T(step, n, kind, (u * P, (u + 1) * P), src)
                            last.then_inc(ring_full, 1)
                        elif kind == "max":
                            u, j, t, h = step[2:]
                            g = unit_at(n, u)
                            pe.wait_ge(stacked[g % 2], stack_value(g))
                            o = take_ring(step)
                            kh = j if L.kheads == 4 else 0
                            nc.tensor.matmul(o[:, :], qs[0:L.row + 1, g % 2, j, t * P:(t + 1) * P],
                                             ks[0:L.row + 1, g % 2, kh, h * S:(h + 1) * S],
                                             start=True, stop=True).then_inc(ring_full, 1)
                        elif kind == "maxT":
                            g = unit_at(n, step[2])
                            if L.halves == 2:
                                pe.wait_ge(max_done, step[2] + 1)
                            else:
                                wait_moved(pe, ("max", n, step[2], 3, NT - 1, 0))
                            o = take_ring(step)
                            nc.tensor.transpose(o[0:16, 0:P], mcol[:, g % 2, 0, :], ident[:, :]).then_inc(ring_full, 1)
                        elif kind == "score":
                            u, s = step[2:]
                            g, i = unit_at(n, u), SINDEX[step]
                            if s == 0:
                                pe.wait_ge(mrow_in, 32 * (g + 1))
                            if i >= 2:
                                pe.wait_ge(exp_done, i - 1)
                            j, pair = s // (L.kt // 2), s % (L.kt // 2)
                            kh = j if L.kheads == 4 else 0
                            for a in range(2):
                                kt = 2 * pair + a
                                last = nc.tensor.matmul(score_banks[:, 2 * (i % 2) + a, :],
                                                        ks[0:L.row + 3, g % 2, kh, kt * P:(kt + 1) * P],
                                                        qs[0:L.row + 3, g % 2, j, :], start=True, stop=True)
                            last.then_inc(score_full, 1)
                        elif kind == "pv":
                            u, s = step[2:]
                            g, i = unit_at(n, u), SINDEX[("score", n, u, s)]
                            if s == 0:
                                wait_moved(pe, ("v", n, L.kt - 1))
                                if g:
                                    pe.wait_ge(heads_done, g)
                            pe.wait_ge(exp_done, i + 1)
                            j, pair = s // (L.kt // 2), s % (L.kt // 2)
                            rows = slice(32 * j, 32 * j + 32)
                            for a in range(2):
                                kt = 2 * pair + a
                                first, final = kt == 0, kt == L.kt - 1
                                p_ = pt[:, i % PTB, a, :]
                                if n == 1:
                                    last = nc.tensor.matmul(num[rows, :], vone[:, kt, u, :], p_, start=first, stop=final)
                                else:
                                    f0 = u * P + 32 * j
                                    nc.tensor.matmul(num[rows, :], v[:, kt, f0:f0 + 32], p_, start=first, stop=final)
                                    last = nc.tensor.matmul(den[rows, :], ones[:, :], p_, start=first, stop=final)
                            last.then_inc(pv_done, 1)
                        elif kind == "o":
                            t = step[2]
                            need_weight(n, "o")
                            if n == 1:
                                pe.wait_ge(at1_done, NC)
                            else:
                                pe.wait_ge(heads_done, unit_at(n, L.units - 1) + 1)
                            o = take_ring(step)
                            wt = w_ap(n, "o")
                            for c in range(NC):
                                last = nc.tensor.matmul(o[:, :], at[:, c, t * P:(t + 1) * P], wt[:, c, :],
                                                        start=(c == 0), stop=(c == NC - 1))
                            last.then_inc(ring_full, 1)
                        elif kind == "up":
                            f, m = step[2:]
                            need_weight(n, f"up{f}")
                            wait_moved(pe, ("xT", n, "mid", NC - 1))
                            last = project_T(step, n, f"up{f}", (m * P, (m + 1) * P), xT)
                            last.then_inc(ring_full, 1)
                        elif kind == "down":
                            f = step[2]
                            need_weight(n, f"down{f}")
                            wait_moved(pe, ("up", n, f, NC - 1))
                            if f == 0:
                                pe.wait_ge(exp_done, SINDEX[("score", n, L.units - 1, L.slots - 1)] + 1)
                            wt = w_ap(n, f"down{f}")
                            for t in range(NT):
                                for m in range(NC):
                                    last = nc.tensor.matmul(score_banks[:, t, :], wide[:, f % 2, m, t * P:(t + 1) * P], wt[:, m, :],
                                                            start=(f == 0 and m == 0), stop=(f == NFB - 1 and m == NC - 1))
                            last.then_inc(down_done, 1)

                @block.scalar
                def _(act):
                    steps = [0]

                    def own(ins):
                        steps[0] += 1
                        ins.then_inc(by_scalar, 1)
                        act.wait_ge(by_scalar, steps[0])

                    for step in STEPS:
                        kind, n = step[0], step[1] if len(step) > 1 else None
                        L = LAYERS[n] if n in (0, 1, 2, 3) else None
                        if kind in ("xT", "aT"):
                            c = step[-1]
                            wait_ring_full(act, step)
                            dst = xT[:, c, :] if kind == "xT" else wide[:, 0, c, :]
                            if kind == "aT":
                                sc, bi = bias["w2"][:, c:c + 1], bias["b2"][:, c:c + 1]
                                act.wait_ge(pv_done, last_pv(unit_at(1, 7)))
                                act.wait_ge(score_masked, len(N_SCORE1))
                            elif step[2] == "z":
                                sc, bi = bias["w10"][:, c:c + 1], bias["b10"][:, c:c + 1]
                            elif step[2] == "mid" and n == 0:
                                sc, bi = bias["w20"][:, c:c + 1], bias["b20"][:, c:c + 1]
                            elif step[2] == "mid":
                                sc, bi = bias["w3"][:, c:c + 1], 0.0
                            else:
                                sc, bi = 1.0, 0.0
                            fn = ACT.Copy if kind == "xT" and step[2] == "x" else ACT.Identity
                            ins = nc.scalar.activation(dst, ring_bank(step)[:, :], fn, bias=bi, scale=sc)
                            ins.then_inc(free_of(step), 1)
                        elif kind in ("q", "k"):
                            u = step[2]
                            wait_ring_full(act, step)
                            g0 = unit_at(n, 2 * u if (n == 1 and kind == "q") else u)
                            if g0 >= 1:
                                prev = g0 - 1
                                act.wait_ge(stacked[prev % 2], stack_value(prev))
                                if prev:
                                    act.wait_ge(stacked[(prev - 1) % 2], stack_value(prev - 1))
                            if kind == "q" and n == 1:
                                own(nc.scalar.activation(q_full[:, :], ring_bank(step)[:, :], ACT.Identity,
                                                         bias=bq4[:, u:u + 1], scale=0.25))
                                ins = nc.scalar.activation(q_hi[:, :], q_full[:, :], ACT.Copy)
                            else:
                                dst = q_hi[:, :] if kind == "q" else k_hi[:, step[3] * S:(step[3] + 1) * S]
                                if n == 2:
                                    ins = nc.scalar.activation(dst, ring_bank(step)[:, :], ACT.Copy)
                                else:
                                    col = 0 if (n, kind) == (1, "k") else u
                                    ins = nc.scalar.activation(dst, ring_bank(step)[:, :], ACT.Identity,
                                                               bias=bias[f"{kind}{n}"][:, col:col + 1])
                            ins.then_inc(hi_done, 1)
                        elif kind == "score":
                            i = SINDEX[step]
                            if n == 1:
                                act.wait_ge(score_masked, N_SCORE1[step])
                            else:
                                act.wait_ge(score_full, i + 1)
                            if i >= PTB:
                                act.wait_ge(pv_done, i - PTB + 1)
                            nc.scalar.activation(pt[:, i % PTB], score_banks[:, 2 * (i % 2):2 * (i % 2) + 2, :], ACT.Exp,
                                                 scale=L.scale).then_inc(exp_done, 1)
                        elif kind == "up":
                            f, m = step[2:]
                            wait_ring_full(act, step)
                            if f >= 2:
                                act.wait_ge(down_done, N_DOWN[("down", n, f - 2)])
                            nc.scalar.activation(wide[:, f % 2, m, :], ring_bank(step)[:, :], ACT.Gelu_apprx_tanh,
                                                 bias=bup[n][:, f * NC + m:f * NC + m + 1]).then_inc(free_of(step), 1)

                @block.vector
                def _(dve):
                    steps = [0]

                    def own(ins):
                        steps[0] += 1
                        ins.then_inc(by_vector, 1)
                        dve.wait_ge(by_vector, steps[0])

                    dve.wait_ge(keymask_in, 48)
                    own(nc.vector.tensor_scalar(mtmp, m8[:, :], 0.0, 1.0, ALU.not_equal, ALU.subtract))
                    own(nc.vector.tensor_scalar(krow[0:1, 0, :], mtmp, -MASKED, None, ALU.mult))
                    own(nc.vector.tensor_scalar(mtmp, m32, 0.0, 1.0, ALU.not_equal, ALU.subtract))
                    own(nc.vector.tensor_scalar(krow[0:1, 1, :], mtmp, -MASKED, None, ALU.mult))
                    nc.vector.tensor_scalar(mcolk[:, :], m8c[:, :], 0.0, None, ALU.not_equal).then_inc(keymask_set, 1)

                    def norm(step):
                        _, n, what = step
                        eps = LAYERS[n].eps
                        if what == "ctx":
                            dve.wait_ge(ctx_in, 32)
                        if what == "x":
                            dve.wait_ge(x_in, 16)
                        if what in ("mid", "out"):
                            wait_moved(dve, ("o", n, NT - 1))
                        src = cx if what == "ctx" else (v if (n, what) == (3, "mid") else x)
                        dst = x if what == "out" else zrow
                        for t in range(NT):
                            own(nc.vector.bn_stats(stats[:, t, :], src[:, t, :]))
                        for t in range(NT):
                            own(nc.vector.bn_aggr(mv[:, t, :], stats[:, t, :]))
                        if n == 3:
                            own(nc.vector.tensor_tensor(var[:, :], mv[:, :, 0], mv[:, :, 0], ALU.mult))
                            own(nc.vector.tensor_tensor(var[:, :], var[:, :], mv[:, :, 1], ALU.add))
                            nc.vector.tensor_scalar(var[:, :], var[:, :], eps, None, ALU.add).then_inc(var_done, 1)
                        else:
                            nc.vector.tensor_scalar(var[:, :], mv[:, :, 1], eps, None, ALU.add).then_inc(var_done, 1)
                        dve.wait_ge(rstd_done, N_NORM[step])
                        for t in range(NT):
                            if n == 3:
                                ins = nc.vector.tensor_scalar(dst[:, t, :], src[:, t, :], rstd[:, t:t + 1], None, ALU.mult)
                            else:
                                ins = nc.vector.tensor_scalar(dst[:, t, :], src[:, t, :], mv[:, t, 0:1], rstd[:, t:t + 1],
                                                              ALU.subtract, ALU.mult)
                            own(ins)
                            if n == 1:
                                own(nc.vector.tensor_tensor(x[:, t, :], x[:, t, :], row["gamma1"][:, :], ALU.mult))
                                own(nc.vector.tensor_tensor(x[:, t, :], x[:, t, :], row["beta1"][:, :], ALU.add))
                        dve.sem_inc(norm_done, 1)

                    for step in STEPS:
                        kind, n = step[0], step[1] if len(step) > 1 else None
                        L = LAYERS[n] if n in (0, 1, 2, 3) else None
                        if kind in RINGED:
                            bank = ring_bank(step)
                        if kind == "norm":
                            norm(step)
                        elif kind in ("ctxT", "maskT"):
                            wait_ring_full(dve, step)
                            dst = ctxT[:, step[1], :] if kind == "ctxT" else wide[:, 1, step[1], :]
                            nc.vector.tensor_copy(dst, bank[:, :]).then_inc(free_of(step), 1)
                        elif kind == "v":
                            t = step[2]
                            wait_ring_full(dve, step)
                            if n == 1:
                                ins = nc.vector.tensor_tensor(vone[:, t, :, 0:16],
                                                              bank[:, 0:128].rearrange("p (g d) -> p g d", g=8),
                                                              row["v1"][:, :].rearrange("p (g d) -> p g d", g=8), ALU.add)
                            elif n == 2:
                                ins = nc.vector.tensor_scalar(v[:, t, :], bank[:, :], mcolk[:, t:t + 1], None, ALU.mult)
                            else:
                                ins = nc.vector.tensor_tensor(v[:, t, :], bank[:, :], row[f"v{n}"][:, :], ALU.add)
                            ins.then_inc(free_of(step), 1)
                        elif kind in ("q", "k"):
                            u = step[2]
                            dve.wait_ge(hi_done, N_QK[step])
                            if kind == "q" and n == 1:
                                ins = nc.vector.tensor_tensor(q_lo[:, :], q_full[:, :], q_hi[:, :].bitcast(F32), ALU.subtract)
                            else:
                                if kind == "q":
                                    dst, hi = q_lo[:, :], q_hi[:, :]
                                else:
                                    h = slice(step[3] * S, (step[3] + 1) * S)
                                    dst, hi = k_lo[:, h], k_hi[:, h]
                                if n == 2:
                                    ins = nc.vector.tensor_tensor(dst, bank[:, :], hi.bitcast(F32), ALU.subtract)
                                else:
                                    col = 0 if (n, kind) == (1, "k") else u
                                    ins = nc.vector.scalar_tensor_tensor(out=dst, in0=bank[:, :],
                                                                         scalar=bias[f"{kind}{n}"][:, col:col + 1],
                                                                         in1=hi.bitcast(F32), op0=ALU.add, op1=ALU.subtract)
                            ins.then_inc(free_of(step), 1)
                        elif kind == "max":
                            u, j, t, h = step[2:]
                            g = unit_at(n, u)
                            wait_ring_full(dve, step)
                            col = mcol[:, g % 2, h, 4 * j + t:4 * j + t + 1]
                            if n == 1:
                                ins = nc.vector.tensor_tensor_reduce(bank[:, :], bank[:, :], wide[:, 0, t, :], 1.0, LOWEST,
                                                                     ALU.add, ALU.max, col)
                            else:
                                ins = nc.vector.tensor_reduce(col, bank[:, :], AX.X, ALU.max)
                            ins.then_inc(free_of(step), 1)
                            if L.halves == 2 and (j, t, h) == (3, NT - 1, 1):
                                wait_moved(dve, step)
                                nc.vector.tensor_tensor(mcol[:, g % 2, 0, :], mcol[:, g % 2, 0, :],
                                                        mcol[:, g % 2, 1, :], ALU.max).then_inc(max_done, 1)
                        elif kind == "maxT":
                            g = unit_at(n, step[2])
                            wait_ring_full(dve, step)
                            if g:
                                dve.wait_ge(mrow_in, 32 * g)
                            own(nc.vector.tensor_scalar(nm_hi[:, :], bank[0:16, 0:P], -1.0, None, ALU.mult))
                            nc.vector.scalar_tensor_tensor(out=nm_lo[:, :], in0=bank[0:16, 0:P], scalar=-1.0,
                                                           in1=nm_hi[:, :].bitcast(F32), op0=ALU.mult, op1=ALU.subtract
                                                           ).then_inc(free_of(step), 1)
                        elif kind == "score" and n == 1:
                            i, s = SINDEX[step], step[3]
                            dve.wait_ge(score_full, i + 1)
                            if i == SINDEX[("score", 1, 0, 0)]:
                                wait_moved(dve, ("maskT", NT - 1))
                            pair = s % 2
                            banks2 = score_banks[:, 2 * (i % 2):2 * (i % 2) + 2, :]
                            nc.vector.tensor_tensor(banks2, banks2, wide[:, 1, 2 * pair:2 * pair + 2, :], ALU.add
                                                    ).then_inc(score_masked, 1)
                        elif kind == "heads":
                            u = step[2]
                            g = unit_at(n, u)
                            dve.wait_ge(pv_done, last_pv(g))
                            if n == 1:
                                if u:
                                    dve.wait_ge(heads1_moved, 128 * u)
                                nc.vector.tensor_copy(heads1[:, :], num[:, :]).then_inc(heads_done, 1)
                                if u % 2:
                                    dve.wait_ge(heads1_moved, 128 * (u + 1))
                                    own(nc.vector.reciprocal(rden[:, :], rden[:, :]))
                                    nc.vector.tensor_tensor(at[:, u // 2, :], at[:, u // 2, :], rden[:, :], ALU.mult
                                                            ).then_inc(at1_done, 1)
                            else:
                                own(nc.vector.reciprocal(rden[:, :], den[:, :]))
                                nc.vector.tensor_tensor(at[:, u, :], num[:, :], rden[:, :], ALU.mult).then_inc(heads_done, 1)
                        elif kind == "o":
                            t = step[2]
                            wait_ring_full(dve, step)
                            if n == 2:
                                ins = nc.vector.scalar_tensor_tensor(out=x[:, t, :], in0=bank[:, :], scalar=gtanh[:, 0:1],
                                                                     in1=x[:, t, :], op0=ALU.mult, op1=ALU.add)
                            else:
                                dst = v[:, t, :] if n == 3 else x[:, t, :]
                                own(nc.vector.tensor_tensor(bank[:, :], bank[:, :], row[f"o{n}"][:, :], ALU.add))
                                ins = nc.vector.tensor_tensor(dst, bank[:, :], x[:, t, :], ALU.add)
                            ins.then_inc(free_of(step), 1)
                        elif kind == "mlp_out":
                            dve.wait_ge(down_done, N_DOWN[("down", n, NFB - 1)])
                            for t in range(NT):
                                own(nc.vector.tensor_tensor(score_banks[:, t, :], score_banks[:, t, :], row[f"down{n}"][:, :], ALU.add))
                                own(nc.vector.tensor_tensor(x[:, t, :], score_banks[:, t, :], x[:, t, :], ALU.add))
                            dve.sem_inc(mlp_done, 1)
            for s in sems:
                nc.sync.sem_clear(s)
            nc.all_engine_barrier()


_F32 = ["x", "ctx_2048", "mask_Bx1xSxS2_ff0"]
_VECS = ["L0_xattn_ln1_w", "L0_xattn_ln1_b", "L0_xattn_q_b", "L0_xattn_k_b", "L0_xattn_v_b", "L0_xattn_cproj_b",
         "L0_xattn_ln2_w", "L0_xattn_ln2_b", "L0_xattn_fc_b", "L0_xattn_proj_b", "L1_xattn_bq", "L1_xattn_bk",
         "L1_xattn_bv", "L1_xattn_bo", "L1_xattn_gamma", "L1_xattn_beta", "L2_xattn_ln_gamma",
         "L2_xattn_ln_beta", "L2_xattn_gate", "L3_xattn_q_b", "L3_xattn_out_b", "L3_xattn_postnorm_w",
         "L3_xattn_mlp_b1", "L3_xattn_mlp_b2"]
_BY_PARTITION = ["L0_xattn_q_b", "L0_xattn_k_b", "L1_xattn_bq", "L1_xattn_bk", "L3_xattn_q_b", "L3_k_b",
                 "L0_xattn_ln1_w", "L0_xattn_ln1_b", "L0_xattn_ln2_w", "L0_xattn_ln2_b", "L2_xattn_ln_gamma",
                 "L2_xattn_ln_beta", "L3_xattn_postnorm_w", "L0_xattn_fc_b", "L3_xattn_mlp_b1"]
_WEIGHTS = {"q0": "L0_xattn_q_w", "k0": "L0_xattn_k_w", "v0": "L0_xattn_v_w", "o0": "L0_xattn_cproj_w",
            "up0": "L0_xattn_fc_w", "down0": "L0_xattn_proj_w", "q1": "L1_xattn_Wq", "k1": "L1_xattn_Wk",
            "v1": "L1_xattn_Wv", "o1": "L1_xattn_Wo", "q3": "L3_xattn_q_w", "o3": "L3_xattn_out_w",
            "up3": "L3_xattn_mlp_w1", "down3": "L3_xattn_mlp_w2"}


def kernel(**inputs):
    import numpy as np
    import concourse.bacc as bacc
    from concourse.bass_utils import run_bass_kernel_spmd as run

    a = {k: np.ascontiguousarray(inputs[k]) for k in _F32 + _VECS + ["mask_BxS2_ik0"]}
    a["mask8"] = np.ascontiguousarray(inputs["mask_BxS2_bf1"]).view(np.uint8)
    a["mask8_cols"] = np.ascontiguousarray(a["mask8"].reshape(B, NT, P).transpose(0, 2, 1))
    for k, name in _WEIGHTS.items():
        a[k] = np.ascontiguousarray(inputs[name])
    for k, name in (("q2", "L2_xattn_Wq"), ("k2", "L2_xattn_Wk"), ("v2", "L2_xattn_Wv"), ("o2", "L2_xattn_Wo")):
        a[k] = np.ascontiguousarray(np.asarray(inputs[name]).T)
    kv_w, kv_b = np.asarray(inputs["L3_xattn_kv_w"]), np.asarray(inputs["L3_xattn_kv_b"])
    a["k3"], a["v3"] = np.ascontiguousarray(kv_w[:, 0::2]), np.ascontiguousarray(kv_w[:, 1::2])
    a["L3_k_b"], a["L3_v_b"] = np.ascontiguousarray(kv_b[0::2]), np.ascontiguousarray(kv_b[1::2])

    for k in _BY_PARTITION:
        a[k] = np.ascontiguousarray(a[k].reshape(-1, P).T)

    nc = bacc.Bacc("TRN2", target_bir_lowering=False, num_devices=1)
    arrays, args = {}, {}
    for k, arr in a.items():
        arrays[f"in_{k}"] = arr
        args[k] = nc.dram_tensor(f"in_{k}", arr.shape, mybir.dt.from_np(arr.dtype), kind="ExternalInput").ap()
    out = nc.dram_tensor("out_0", (B, S, D), F32, kind="ExternalOutput").ap()
    build(nc, args, out)
    r = run(nc, [arrays], core_ids=[0])
    return r.results[0]["out_0"]
```

```python
from contextlib import ExitStack

import numpy as np

import concourse.bass as bass
from concourse import mybir

ALU = mybir.AluOpType
ACT = mybir.ActivationFunctionType
AX = mybir.AxisListType
F32 = mybir.dt.float32
F32R = mybir.dt.float32r
U8 = mybir.dt.uint8
I32 = mybir.dt.int32

P = 128
B, S, D = 4, 512, 512
NT = S // P
NC = D // P
NFB = 4
MASKED = -(2.0 ** 100)
LOWEST = float(np.finfo(np.float32).min)
WSLOTS = 3
UB = 3
PTB = 3
RING = 2


class Layer:
    def __init__(self, n, hd, units, keys, scale, eps, vcols):
        self.n, self.hd, self.units, self.keys, self.scale, self.eps = n, hd, units, keys, scale, eps
        self.copies = 3 if hd == 32 else 4
        self.row = self.copies * hd
        self.kt = keys // P
        self.halves = keys // S
        self.slots = 4 * self.kt // 2
        self.kheads = 4 if hd == 32 else 1
        self.vcols = vcols


LAYERS = [
    Layer(0, 32, 4, 512, 32 ** -0.5, 1e-5, 512),
    Layer(1, 16, 8, 512, 1.0, 1e-6, 128),
    Layer(2, 32, 4, 512, 32 ** -0.5, 1e-5, 512),
    Layer(3, 32, 4, 1024, 1.0 / 32, 1e-6, 512),
]
UNITS = [(L.n, u) for L in LAYERS for u in range(L.units)]

WEIGHTS = []
for _n in range(4):
    WEIGHTS += [(_n, w) for w in (("k", "v", "q", "o") if _n == 1 else ("v", "q", "k", "o"))]
    if _n in (0, 3):
        WEIGHTS += [(_n, f"{w}{f}") for f in range(NFB) for w in ("up", "down")]
WINDEX = {w: i for i, w in enumerate(WEIGHTS)}


def layer_steps(L):
    n = L.n

    def project(u):
        out = []
        if n != 1 or u % 2 == 0:
            out.append(("q", n, u if n != 1 else u // 2))
        if n != 1 or u == 0:
            out += [("k", n, u, h) for h in range(L.halves)]
        return out + [("stack", n, u)]

    def maxima(u):
        return [("max", n, u, j, t, h) for j in range(4) for t in range(NT) for h in range(L.halves)] + [("maxT", n, u)]

    steps = []
    if n == 0:
        steps += [("ctxT", c) for c in range(NC)]
        steps += [("norm", 0, "x")] + [("xT", 0, "z", c) for c in range(NC)]
    elif n == 1:
        steps += [("mask_in",)] + [("xT", 1, "x", c) for c in range(NC)] + [("maskT", t) for t in range(NT)]
    elif n == 2:
        steps += [("norm", 2, "ctx")] + [("aT", c) for c in range(NC)] + [("xT", 2, "x", c) for c in range(NC)]
    else:
        steps += [("xT", 3, "x", c) for c in range(NC)]
    steps += project(0) + project(1) + [("v", n, t) for t in range(L.kt)] + maxima(0) + project(2)
    for u in range(L.units):
        fill = (maxima(u + 1) if u + 1 < L.units else [])
        fill += (project(u + 2) if 1 <= u < L.units - 2 else [])
        done = 0
        steps.append(("score", n, u, 0))
        for s in range(L.slots):
            if s + 1 < L.slots:
                steps.append(("score", n, u, s + 1))
            upto = len(fill) * (s + 1) // L.slots
            steps += fill[done:upto]
            done = upto
            steps.append(("pv", n, u, s))
        steps += [("heads", n, u)]
    steps += [("o", n, t) for t in range(NT)]
    if n in (0, 3):
        steps += [("norm", n, "mid")] + [("xT", n, "mid", c) for c in range(NC)]
        for f in range(NFB):
            steps += [("up", n, f, m) for m in range(NC)]
            if f:
                steps.append(("down", n, f - 1))
        steps += [("down", n, NFB - 1), ("mlp_out", n)]
    elif n == 1:
        steps += [("norm", 1, "out")]
    return steps


STEPS = [s for L in LAYERS for s in layer_steps(L)]
RINGED = ("ctxT", "xT", "aT", "maskT", "v", "q", "k", "max", "maxT", "o", "up")
RING_STEPS = [s for s in STEPS if s[0] in RINGED]
RINDEX = {s: i for i, s in enumerate(RING_STEPS)}
SCORE_STEPS = [s for s in STEPS if s[0] == "score"]
SINDEX = {s: i for i, s in enumerate(SCORE_STEPS)}


def last_use():
    out = {}
    for i, (n, name) in enumerate(WEIGHTS):
        if name[:2] == "up":
            out["up", n, int(name[2:]), NC - 1] = i
        elif name[:4] == "down":
            out["down", n, int(name[4:])] = i
        else:
            out[[s for s in STEPS if s[:2] == (name, n)][-1]] = i
    return out


LAST_USE = last_use()


def order(kinds):
    return {s: i + 1 for i, s in enumerate([s for s in STEPS if s[0] in kinds])}


def build(nc, A, out):
    ctx = ExitStack()

    def sb(name, shape, dt=F32):
        return ctx.enter_context(nc.sbuf_tensor(name, shape, dt))

    def sem(name):
        s = ctx.enter_context(nc.semaphore(name))
        sems.append(s)
        return s

    with ctx:
        sems = []
        w = sb("w", [P, WSLOTS, NC, D])
        x = sb("x", [P, NT, D])
        ctxT = sb("ctxT", [P, NC, S])
        xT = sb("xT", [P, NC, S])
        at = sb("at", [P, NC, S])
        v = sb("v", [P, 8, D])
        cx = v[:, 0:NT, :]
        wide = sb("wide", [P, 2, NC, D])
        qs = sb("qs", [P, UB, 4, S], F32R)
        ks = sb("ks", [P, UB, 2, 4, S], F32R)
        k_hi, k_lo, q_hi, q_lo = (ks[:, 0, 1, i, :] for i in range(4))
        q_full = sb("q_full", [P, S])
        pt = sb("pt", [P, PTB, 2, S])
        rden = sb("rden", [P, S])
        denT = sb("denT", [P, S])
        heads1 = denT
        vone = sb("vone", [P, NT, 8, 32])
        mcol = sb("mcol", [P, 2, 2, 16])
        nm_hi = sb("nm_hi", [16, P], F32R)
        nm_lo = sb("nm_lo", [16, P], F32R)
        krow = sb("krow", [3, 3, S], F32R)
        m8 = sb("m8", [1, S], U8)
        m32 = rden[0:1, :].bitcast(I32)
        mtmp = q_full[0:1, :]
        mcolk = sb("mcolk", [P, NT])
        m8c = sb("m8c", [P, NT], U8)
        ones = sb("ones", [P, 32])
        ident = sb("ident", [P, P])
        stats = sb("stats", [P, NT, 6])
        mv = sb("mv", [P, NT, 2])
        rstd = sb("rstd", [P, NT])
        var = sb("var", [P, NT])
        minus_half = sb("minus_half", [P, NT])
        gate = sb("gate", [P, 1])
        gtanh = sb("gtanh", [P, 1])
        bias32 = {k: sb(f"c_{k}", [32, 4 * NC]) for k in ("q0", "k0", "q3", "k3")}
        bias = {k: sb(f"c_{k}", [P, NC]) for k in
                ("q1", "w10", "b10", "w20", "b20", "w2", "b2", "w3")}
        bias["k1"] = sb("c_k1", [P, 1])
        bq4 = sb("bq4", [P, NC])
        bup = {0: sb("c_up0", [P, NFB * NC]), 3: sb("c_up3", [P, NFB * NC])}
        row = {k: sb(f"r_{k}", [P, D]) for k in
               ("v0", "o0", "down0", "o1", "v3", "o3", "down3")}
        row["gamma1"], row["beta1"] = pt[:, 0, 0, :], pt[:, 0, 1, :]
        row["v1"] = sb("r_v1", [P, 128])

        banks = [ctx.enter_context(nc.psum_tensor(f"bank{i}", [P, 512], F32)) for i in range(4, 8)]
        score_banks = ctx.enter_context(nc.psum_tensor("score_banks", [P, 4, 512], F32))
        ring = banks[0:2]
        num, den = banks[2], banks[3]

        const_in = ctx.enter_context(nc.semaphore("const_in"))
        const_set = ctx.enter_context(nc.semaphore("const_set"))
        gate_set = ctx.enter_context(nc.semaphore("gate_set"))
        rows_in = ctx.enter_context(nc.semaphore("rows_in"))
        x_in, ctx_in, mask_in, out_stored = sem("x_in"), sem("ctx_in"), sem("mask_in"), sem("out_stored")
        keymask_in = sem("keymask_in")
        keymask_set = sem("keymask_set")
        w_in = [sem(f"w_in{i}") for i in range(WSLOTS)]
        ring_full = sem("ring_full")
        ring_free = [sem(f"ring_free{i}") for i in range(RING)]
        by_vector = sem("by_vector")
        by_scalar = sem("by_scalar")
        norm_done = sem("norm_done")
        var_done, rstd_done = sem("var_done"), sem("rstd_done")
        hi_done = sem("hi_done")
        stacked = [sem(f"stacked{i}") for i in range(UB)]
        sums_out, values_out = sem("sums_out"), sem("values_out")
        rden_done, at_done = sem("rden_done"), sem("at_done")
        gamma_in = sem("gamma_in")
        max_done = sem("max_done")
        mrow_in = sem("mrow_in")
        score_full, score_masked = sem("score_full"), sem("score_masked")
        exp_done, pv_done = sem("exp_done"), sem("pv_done")
        heads_done = sem("heads_done")
        heads1_moved = sem("heads1_moved")
        down_done = sem("down_done")
        mlp_done = sem("mlp_done")

        N_NORM = order(("norm",))
        N_QK = order(("q", "k"))
        N_MAXT, N_SCORE, N_PV = order(("maxT",)), order(("score",)), order(("pv",))
        N_DOWN, N_MLP = order(("down",)), order(("mlp_out",))
        N_SCORE1 = {s: i + 1 for i, s in enumerate([s for s in SCORE_STEPS if s[1] == 1])}

        def unit_at(n, u):
            return UNITS.index((n, u))

        def stack_dmas(g):
            n, u = UNITS[g]
            L = LAYERS[n]
            rows = u < UB and n != 2
            if n == 1:
                return (4 + L.kheads) * L.copies + 2 * rows
            return 1 + L.halves + L.halves * rows

        def wait_stacked(eng, g):
            eng.wait_ge(stacked[g % UB], 16 * sum(stack_dmas(i) for i in range(g % UB, g + 1, UB)))

        def last_pv(g):
            n, u = UNITS[g]
            return N_PV[("pv", n, u, LAYERS[n].slots - 1)]

        def at_count(g):
            return sum(1 for n, u in UNITS[:g + 1] if n != 1 or u % 2)

        def last_project(n, u):
            if n == 1:
                return max(("q", 1, u // 2), ("k", 1, 0, 0), key=RINDEX.get)
            return ("k", n, u, LAYERS[n].halves - 1)

        def ring_bank(step):
            return ring[RINDEX[step] % RING]

        def wait_ring_full(eng, step):
            eng.wait_ge(ring_full, RINDEX[step] + 1)

        def free_of(step):
            return ring_free[RINDEX[step] % RING]

        def wait_moved(eng, step):
            for i in range(max(RINDEX[step] - RING + 1, 0), RINDEX[step] + 1):
                eng.wait_ge(ring_free[i % RING], i // RING + 1)

        def wait_weights_used(eng, n, name):
            step = [s for s, i in LAST_USE.items() if WEIGHTS[i] == (n, name)][0]
            if step[0] == "down":
                eng.wait_ge(down_done, N_DOWN[step])
            else:
                wait_ring_full(eng, step)

        def w_ap(n, name):
            return w[:, WINDEX[(n, name)] % WSLOTS]

        def bcast(ap, cols):
            return ap.rearrange("(o n) -> o n", o=1).broadcast_to([P, cols])

        zrow = at

        CONSTS = []
        for key, name in (("q0", "L0_xattn_q_b"), ("k0", "L0_xattn_k_b"), ("q3", "L3_xattn_q_b"), ("k3", "L3_k_b")):
            CONSTS.append((bias32[key][:, :], A[name]))
        for key, name in (("q1", "L1_xattn_bq"), ("k1", "L1_xattn_bk"), ("w10", "L0_xattn_ln1_w"),
                          ("b10", "L0_xattn_ln1_b"), ("w20", "L0_xattn_ln2_w"), ("b20", "L0_xattn_ln2_b"),
                          ("w2", "L2_xattn_ln_gamma"), ("b2", "L2_xattn_ln_beta"), ("w3", "L3_xattn_postnorm_w")):
            CONSTS.append((bias[key][:, :], A[name]))
        CONSTS.append((bup[0][:, :], A["L0_xattn_fc_b"]))
        CONSTS.append((bup[3][:, :], A["L3_xattn_mlp_b1"]))
        for key, name in (("v0", "L0_xattn_v_b"), ("o0", "L0_xattn_cproj_b"), ("down0", "L0_xattn_proj_b"),
                          ("v1", "L1_xattn_bv"), ("o1", "L1_xattn_bo"), ("v3", "L3_v_b"), ("o3", "L3_xattn_out_b"),
                          ("down3", "L3_xattn_mlp_b2")):
            CONSTS.append((row[key][:, :], bcast(A[name], row[key].shape[1])))
        CONSTS.append((gate[:, :], bcast(A["L2_xattn_gate"], 1)))

        with nc.Block() as block:
            @block.sync
            def _(sp):
                for dst, src in CONSTS:
                    sp.dma_start(dst, src, allow_slow_non_contiguous=True).then_inc(const_in, 16)
                sp.wait_ge(const_set, 5)
                for i in range(UB):
                    sp.dma_start(qs[96:97, i].bitcast(F32), krow[1:2, 0:1, :].bitcast(F32).broadcast_to([1, 4, S])
                                 ).then_inc(rows_in, 16)
                sp.wait_ge(rows_in, 16 * UB)

            @block.gpsimd
            def _(pool):
                nc.gpsimd.memset(ident[:, :], 0.0).then_inc(const_set, 1)
                nc.gpsimd.memset(ones[:, :], 1.0).then_inc(const_set, 1)
                nc.gpsimd.memset(krow[:, :, :].bitcast(F32), 1.0).then_inc(const_set, 1)
                nc.gpsimd.memset(vone[:, :, :, :], 1.0).then_inc(const_set, 1)
                nc.gpsimd.memset(minus_half[:, :], -0.5).then_inc(const_set, 1)
                pool.wait_ge(const_set, 5)
                nc.gpsimd.affine_select(out=ident[:, :], in_=ident[:, :], compare_op=ALU.not_equal, fill=1.0,
                                        base=0, pattern=[[-1, P]], channel_multiplier=1).then_inc(const_set, 1)
                nc.gpsimd.memset(krow[0:1, 2:3, :].bitcast(F32), 0.0).then_inc(const_set, 1)

            @block.scalar
            def _(act):
                act.wait_ge(const_in, 16 * len(CONSTS))
                nc.scalar.activation(gtanh[:, :], gate[:, :], ACT.Tanh).then_inc(gate_set, 1)
                nc.scalar.activation(bq4[:, :], bias["q1"][:, :], ACT.Copy, scale=0.25).then_inc(gate_set, 1)

            @block.vector
            def _(dve):
                dve.wait_ge(const_in, 16 * len(CONSTS))
                dve.wait_ge(const_set, 7)
                dve.wait_ge(gate_set, 2)

        with nc.Fori(0, B) as b:
            block = nc.Block()
            with block:
                @block.sync
                def _(sp):
                    def tokens(ap):
                        return ap[bass.ds(b, 1)].rearrange("o (t p) d -> p (o t) d", p=P)

                    def load_weights(i):
                        n, name = WEIGHTS[i]
                        if i >= WSLOTS:
                            wait_weights_used(sp, *WEIGHTS[i - WSLOTS])
                        if name[:2] == "up":
                            f = int(name[2:])
                            src = A[f"up{n}"][:, f * D:(f + 1) * D]
                        elif name[:4] == "down":
                            f = int(name[4:])
                            src = A[f"down{n}"][f * D:(f + 1) * D, :]
                        else:
                            src = A[f"{name}{n}"]
                        sp.dma_start(w[:, i % WSLOTS, :, 0:src.shape[1]], src.rearrange("(c p) n -> p c n", p=P)
                                       ).then_inc(w_in[i % WSLOTS], 16)

                    sp.dma_start(cx, tokens(A["ctx_2048"])).then_inc(ctx_in, 16)
                    sp.dma_start(x[:, :, :], tokens(A["x"])).then_inc(x_in, 16)
                    sp.dma_start(m8[:, :], A["mask8"][bass.ds(b, 1), :]).then_inc(keymask_in, 16)
                    sp.dma_start(m32, A["mask_BxS2_ik0"][bass.ds(b, 1), :]).then_inc(keymask_in, 16)
                    sp.dma_start(m8c[:, :], A["mask8_cols"][bass.ds(b, 1)].rearrange("o p t -> p (o t)")
                                 ).then_inc(keymask_in, 16)
                    for i in range(WSLOTS):
                        load_weights(i)
                    sp.wait_ge(keymask_set, 1)
                    for step in STEPS:
                        kind, n = step[0], step[1] if len(step) > 1 else None
                        if kind == "mask_in":
                            sp.wait_ge(pv_done, last_pv(unit_at(0, 3)))
                            sp.dma_start(cx, tokens(A["ctx_2048"])).then_inc(ctx_in, 16)
                            sp.wait_ge(mlp_done, N_MLP[("mlp_out", 0)])
                            sp.dma_start(wide[:, 0], A["mask_Bx1xSxS2_ff0"][bass.ds(b, 1)].rearrange(
                                "o a (t p) k -> p (o a t) k", p=P)).then_inc(mask_in, 16)
                        elif kind == "stack":
                            u, L = step[2], LAYERS[n]
                            g, hd, cp = unit_at(n, u), L.hd, L.copies
                            gb, done = g % UB, stacked[g % UB]
                            wait_moved(sp, last_project(n, u))
                            if n == 1:
                                sp.wait_ge(pv_done, last_pv(g - UB))
                                for i in range(cp):
                                    part = (q_hi, q_lo)[i % 2]
                                    for j in range(4):
                                        r = 64 * (u % 2) + j * hd
                                        sp.dma_start(qs[hd * i:hd * (i + 1), gb, j].bitcast(F32),
                                                     part[r:r + hd, :].bitcast(F32)).then_inc(done, 16)
                                    part = (k_hi, k_hi, k_lo, k_lo)[i]
                                    sp.dma_start(ks[hd * i:hd * (i + 1), gb, 0, 0].bitcast(F32),
                                                 part[hd * u:hd * (u + 1), :].bitcast(F32)).then_inc(done, 16)
                                if u < UB:
                                    sp.dma_start(qs[L.row:L.row + 1, gb].bitcast(F32),
                                                 krow[1:2, 0:1, :].bitcast(F32).broadcast_to([1, 4, S])).then_inc(done, 16)
                                    sp.dma_start(ks[L.row:L.row + 3, gb, 0, 0:1].bitcast(F32),
                                                 krow[:, 2:3, :].bitcast(F32)).then_inc(done, 16)
                            else:
                                sp.dma_start(qs[2 * hd:3 * hd, gb].bitcast(F32), qs[0:hd, gb].bitcast(F32)).then_inc(done, 16)
                                for h in range(L.halves):
                                    sp.dma_start(ks[hd:2 * hd, gb, h].bitcast(F32), ks[0:hd, gb, h].bitcast(F32)
                                                 ).then_inc(done, 16)
                                if u < UB and n != 2:
                                    if g >= UB:
                                        sp.wait_ge(pv_done, last_pv(g - UB))
                                    for h, which in enumerate((0,) if n == 0 else (1, 2)):
                                        sp.dma_start(ks[L.row:L.row + 3, gb, h].bitcast(F32),
                                                     krow[:, which:which + 1, :].bitcast(F32).broadcast_to([3, 4, S])
                                                     ).then_inc(done, 16)
                        elif kind == "maxT":
                            u, L = step[2], LAYERS[n]
                            g = unit_at(n, u)
                            wait_moved(sp, step)
                            for i, part in enumerate((nm_hi, nm_lo)):
                                sp.dma_start(qs[L.row + 1 + i:L.row + 2 + i, g % UB].bitcast(F32).rearrange(
                                    "o j (t n) -> o (j t) n", n=P), part[:, :].bitcast(F32)).then_inc(mrow_in, 16)
                        elif kind == "heads" and n == 1:
                            u = step[2]
                            sp.wait_ge(heads_done, u + 1)
                            if u % 2 == 0:
                                sp.wait_ge(at_done, at_count(unit_at(1, u) - 1))
                            r = 64 * (u % 2)
                            for j in range(4):
                                sp.dma_start(at[r + 16 * j:r + 16 * j + 16, u // 2, :],
                                             heads1[32 * j:32 * j + 16, :]).then_inc(heads1_moved, 16)
                                sp.dma_start(rden[r + 16 * j:r + 16 * j + 16, :],
                                             heads1[32 * j + 16:32 * j + 32, :]).then_inc(heads1_moved, 16)
                            if u == LAYERS[1].units - 1:
                                sp.wait_ge(pv_done, last_pv(unit_at(1, u)))
                                sp.dma_start(row["gamma1"], bcast(A["L1_xattn_gamma"], D)).then_inc(gamma_in, 16)
                                sp.dma_start(row["beta1"], bcast(A["L1_xattn_beta"], D)).then_inc(gamma_in, 16)
                        if step in LAST_USE and LAST_USE[step] + WSLOTS < len(WEIGHTS):
                            load_weights(LAST_USE[step] + WSLOTS)
                    sp.wait_ge(mlp_done, N_MLP[("mlp_out", 3)])
                    sp.dma_start(out[bass.ds(b, 1)].rearrange("o (t p) d -> p (o t) d", p=P), x[:, :, :]
                                 ).then_inc(out_stored, 16)
                    sp.wait_ge(out_stored, 16)

                @block.gpsimd
                def _(pool):
                    for step in STEPS:
                        if step[0] == "norm":
                            pool.wait_ge(var_done, N_NORM[step])
                            nc.gpsimd.tensor_tensor(rstd[:, :], var[:, :], minus_half[:, :], ALU.pow
                                                    ).then_inc(rstd_done, 1)
                        elif step[0] == "heads" and step[1] != 1:
                            _, n, u = step
                            g = unit_at(n, u)
                            units = sum(1 for m, _ in UNITS[:g + 1] if m != 1)
                            pool.wait_ge(values_out, g + 1)
                            pool.wait_ge(rden_done, units)
                            nc.gpsimd.tensor_tensor(at[:, u, :], at[:, u, :], rden[:, :], ALU.mult).then_inc(at_done, 1)

                @block.tensor
                def _(pe):
                    landed = [0]

                    def need_weight(n, name):
                        i = WINDEX[(n, name)]
                        while landed[0] <= i:
                            k = landed[0]
                            pe.wait_ge(w_in[k % WSLOTS], 16 * (k // WSLOTS + 1))
                            landed[0] += 1

                    def take_ring(step):
                        i = RINDEX[step]
                        if i >= RING:
                            pe.wait_ge(ring_free[i % RING], i // RING)
                        return ring[i % RING]

                    def project_T(step, n, name, cols, src, c0=0):
                        o = take_ring(step)
                        wt = w_ap(n, name)
                        for c in range(NC):
                            last = nc.tensor.matmul(o[:, :], wt[:, c, cols[0]:cols[1]], src[:, c, :],
                                                    start=(c == 0), stop=(c == NC - 1))
                        return last

                    for step in STEPS:
                        kind, n = step[0], step[1] if len(step) > 1 else None
                        L = LAYERS[n] if n in (0, 1, 2, 3) else None
                        if kind in ("ctxT", "xT", "aT", "maskT"):
                            if kind == "ctxT":
                                pe.wait_ge(ctx_in, 16)
                                src, c = cx, step[1]
                            elif kind == "xT":
                                src, c = {"x": x, "z": zrow, "mid": zrow}[step[2]], step[3]
                                if step[2] == "z":
                                    pe.wait_ge(norm_done, N_NORM[("norm", 0, "x")])
                                elif step[2] == "mid":
                                    pe.wait_ge(norm_done, N_NORM[("norm", n, "mid")])
                                elif n == 1:
                                    pe.wait_ge(mlp_done, N_MLP[("mlp_out", 0)])
                                elif n == 2:
                                    pe.wait_ge(norm_done, N_NORM[("norm", 1, "out")])
                                else:
                                    wait_moved(pe, ("o", 2, NT - 1))
                            elif kind == "aT":
                                pe.wait_ge(norm_done, N_NORM[("norm", 2, "ctx")])
                                src, c = zrow, step[1]
                            else:
                                pe.wait_ge(mask_in, 16)
                                src, c = wide[:, 0], step[1]
                            o = take_ring(step)
                            for t in range(NT):
                                last = nc.tensor.transpose(o[:, t * P:(t + 1) * P], src[:, t, c * P:(c + 1) * P], ident[:, :])
                            last.then_inc(ring_full, 1)
                        elif kind == "v":
                            t = step[2]
                            need_weight(n, "v")
                            if n == 2:
                                wait_moved(pe, ("aT", NC - 1))
                                src, t0 = wide[:, 0], t
                            elif t < NT:
                                wait_moved(pe, ("ctxT", NC - 1))
                                src, t0 = ctxT, t
                            else:
                                wait_moved(pe, ("xT", 3, "x", NC - 1))
                                src, t0 = xT, t - NT
                            o = take_ring(step)
                            wt = w_ap(n, "v")
                            for c in range(NC):
                                last = nc.tensor.matmul(o[:, 0:L.vcols], src[:, c, t0 * P:(t0 + 1) * P], wt[:, c, 0:L.vcols],
                                                        start=(c == 0), stop=(c == NC - 1))
                            last.then_inc(ring_full, 1)
                        elif kind in ("q", "k"):
                            u = step[2]
                            need_weight(n, kind)
                            if kind == "q":
                                wait_moved(pe, ("xT", n, "z" if n == 0 else "x", NC - 1))
                                src = xT
                            else:
                                if n == 2:
                                    src = wide[:, 0]
                                elif step[3] == 1:
                                    src = xT
                                else:
                                    src = ctxT
                            last = project_T(step, n, kind, (u * P, (u + 1) * P), src)
                            last.then_inc(ring_full, 1)
                        elif kind == "max":
                            u, j, t, h = step[2:]
                            g = unit_at(n, u)
                            wait_stacked(pe, g)
                            o = take_ring(step)
                            kh = j if L.kheads == 4 else 0
                            nc.tensor.matmul(o[:, :], qs[0:L.row + 1, g % UB, j, t * P:(t + 1) * P],
                                             ks[0:L.row + 1, g % UB, h, kh, :],
                                             start=True, stop=True).then_inc(ring_full, 1)
                        elif kind == "maxT":
                            g = unit_at(n, step[2])
                            if L.halves == 2:
                                pe.wait_ge(max_done, step[2] + 1)
                            else:
                                wait_moved(pe, ("max", n, step[2], 3, NT - 1, 0))
                            o = take_ring(step)
                            nc.tensor.transpose(o[0:16, 0:P], mcol[:, g % 2, 0, :], ident[:, :]).then_inc(ring_full, 1)
                        elif kind == "score":
                            u, s = step[2:]
                            g, i = unit_at(n, u), SINDEX[step]
                            if s == 0:
                                pe.wait_ge(mrow_in, 32 * (g + 1))
                            if i >= 2:
                                pe.wait_ge(exp_done, i - 1)
                            j, pair = s // (L.kt // 2), s % (L.kt // 2)
                            kh = j if L.kheads == 4 else 0
                            for a in range(2):
                                kt = 2 * pair + a
                                last = nc.tensor.matmul(score_banks[:, 2 * (i % 2) + a, :],
                                                        ks[0:L.row + 3, g % UB, kt // NT, kh, kt % NT * P:(kt % NT + 1) * P],
                                                        qs[0:L.row + 3, g % UB, j, :], start=True, stop=True)
                            last.then_inc(score_full, 1)
                        elif kind == "pv":
                            u, s = step[2:]
                            g, i = unit_at(n, u), SINDEX[("score", n, u, s)]
                            if s == 0:
                                wait_moved(pe, ("v", n, L.kt - 1))
                                if g:
                                    pe.wait_ge(values_out, g)
                                    sums = sum(1 for m, _ in UNITS[:g] if m != 1)
                                    pe.wait_ge(sums_out, sums)
                            pe.wait_ge(exp_done, i + 1)
                            j, pair = s // (L.kt // 2), s % (L.kt // 2)
                            rows = slice(32 * j, 32 * j + 32)
                            for a in range(2):
                                kt = 2 * pair + a
                                first, final = kt == 0, kt == L.kt - 1
                                p_ = pt[:, i % PTB, a, :]
                                if n == 1:
                                    last = nc.tensor.matmul(num[rows, :], vone[:, kt, u, :], p_, start=first, stop=final)
                                else:
                                    f0 = u * P + 32 * j
                                    nc.tensor.matmul(num[rows, :], v[:, kt, f0:f0 + 32], p_, start=first, stop=final)
                                    last = nc.tensor.matmul(den[rows, :], ones[:, :], p_, start=first, stop=final)
                            last.then_inc(pv_done, 1)
                        elif kind == "o":
                            t = step[2]
                            need_weight(n, "o")
                            pe.wait_ge(at_done, at_count(unit_at(n, L.units - 1)))
                            o = take_ring(step)
                            wt = w_ap(n, "o")
                            for c in range(NC):
                                last = nc.tensor.matmul(o[:, :], at[:, c, t * P:(t + 1) * P], wt[:, c, :],
                                                        start=(c == 0), stop=(c == NC - 1))
                            last.then_inc(ring_full, 1)
                        elif kind == "up":
                            f, m = step[2:]
                            need_weight(n, f"up{f}")
                            wait_moved(pe, ("xT", n, "mid", NC - 1))
                            last = project_T(step, n, f"up{f}", (m * P, (m + 1) * P), xT)
                            last.then_inc(ring_full, 1)
                        elif kind == "down":
                            f = step[2]
                            need_weight(n, f"down{f}")
                            wait_moved(pe, ("up", n, f, NC - 1))
                            if f == 0:
                                pe.wait_ge(exp_done, SINDEX[("score", n, L.units - 1, L.slots - 1)] + 1)
                            wt = w_ap(n, f"down{f}")
                            for t in range(NT):
                                for m in range(NC):
                                    last = nc.tensor.matmul(score_banks[:, t, :], wide[:, f % 2, m, t * P:(t + 1) * P], wt[:, m, :],
                                                            start=(f == 0 and m == 0), stop=(f == NFB - 1 and m == NC - 1))
                            last.then_inc(down_done, 1)

                @block.scalar
                def _(act):
                    steps = [0]

                    def own(ins):
                        steps[0] += 1
                        ins.then_inc(by_scalar, 1)
                        act.wait_ge(by_scalar, steps[0])

                    for step in STEPS:
                        kind, n = step[0], step[1] if len(step) > 1 else None
                        L = LAYERS[n] if n in (0, 1, 2, 3) else None
                        if kind in ("xT", "aT"):
                            c = step[-1]
                            wait_ring_full(act, step)
                            dst = xT[:, c, :] if kind == "xT" else wide[:, 0, c, :]
                            if kind == "aT":
                                sc, bi = bias["w2"][:, c:c + 1], bias["b2"][:, c:c + 1]
                                act.wait_ge(pv_done, last_pv(unit_at(1, 7)))
                                act.wait_ge(score_masked, len(N_SCORE1))
                            elif step[2] == "z":
                                sc, bi = bias["w10"][:, c:c + 1], bias["b10"][:, c:c + 1]
                            elif step[2] == "mid" and n == 0:
                                sc, bi = bias["w20"][:, c:c + 1], bias["b20"][:, c:c + 1]
                            elif step[2] == "mid":
                                sc, bi = bias["w3"][:, c:c + 1], 0.0
                            else:
                                sc, bi = 1.0, 0.0
                            fn = ACT.Copy if kind == "xT" and step[2] == "x" else ACT.Identity
                            ins = nc.scalar.activation(dst, ring_bank(step)[:, :], fn, bias=bi, scale=sc)
                            ins.then_inc(free_of(step), 1)
                        elif kind in ("q", "k"):
                            u = step[2]
                            wait_ring_full(act, step)
                            if n == 1:
                                g0 = unit_at(1, 2 * u if kind == "q" else 0)
                                for g in range(max(g0 - UB, unit_at(1, 0)), g0):
                                    wait_stacked(act, g)
                                if kind == "q":
                                    own(nc.scalar.activation(q_full[:, :], ring_bank(step)[:, :], ACT.Identity,
                                                             bias=bq4[:, u:u + 1], scale=0.25))
                                    ins = nc.scalar.activation(q_hi, q_full[:, :], ACT.Copy)
                                else:
                                    ins = nc.scalar.activation(k_hi, ring_bank(step)[:, :], ACT.Identity,
                                                               bias=bias["k1"][:, 0:1])
                            else:
                                g = unit_at(n, u)
                                if g >= UB:
                                    act.wait_ge(pv_done, last_pv(g - UB))
                                for j in range(4):
                                    dst = qs[0:32, g % UB, j, :] if kind == "q" else ks[0:32, g % UB, step[3], j, :]
                                    src = ring_bank(step)[32 * j:32 * j + 32, :]
                                    if n == 2:
                                        ins = nc.scalar.activation(dst, src, ACT.Copy)
                                    else:
                                        ins = nc.scalar.activation(dst, src, ACT.Identity,
                                                                   bias=bias32[f"{kind}{n}"][:, 4 * u + j:4 * u + j + 1])
                            ins.then_inc(hi_done, 1)
                        elif kind == "score":
                            i = SINDEX[step]
                            if n == 1:
                                act.wait_ge(score_masked, N_SCORE1[step])
                            else:
                                act.wait_ge(score_full, i + 1)
                            if i >= PTB:
                                act.wait_ge(pv_done, i - PTB + 1)
                            nc.scalar.activation(pt[:, i % PTB], score_banks[:, 2 * (i % 2):2 * (i % 2) + 2, :], ACT.Exp,
                                                 scale=L.scale).then_inc(exp_done, 1)
                        elif kind == "heads" and n != 1:
                            g = unit_at(n, step[2])
                            act.wait_ge(pv_done, last_pv(g))
                            nc.scalar.activation(at[:, step[2], :], num[:, :], ACT.Copy).then_inc(values_out, 1)
                        elif kind == "up":
                            f, m = step[2:]
                            wait_ring_full(act, step)
                            if f >= 2:
                                act.wait_ge(down_done, N_DOWN[("down", n, f - 2)])
                            nc.scalar.activation(wide[:, f % 2, m, :], ring_bank(step)[:, :], ACT.Gelu_apprx_tanh,
                                                 bias=bup[n][:, f * NC + m:f * NC + m + 1]).then_inc(free_of(step), 1)

                @block.vector
                def _(dve):
                    steps = [0]

                    def own(ins):
                        steps[0] += 1
                        ins.then_inc(by_vector, 1)
                        dve.wait_ge(by_vector, steps[0])

                    dve.wait_ge(keymask_in, 48)
                    own(nc.vector.tensor_scalar(mtmp, m8[:, :], 0.0, 1.0, ALU.not_equal, ALU.subtract))
                    own(nc.vector.tensor_scalar(krow[0:1, 0, :], mtmp, -MASKED, None, ALU.mult))
                    own(nc.vector.tensor_scalar(mtmp, m32, 0.0, 1.0, ALU.not_equal, ALU.subtract))
                    own(nc.vector.tensor_scalar(krow[0:1, 1, :], mtmp, -MASKED, None, ALU.mult))
                    nc.vector.tensor_scalar(mcolk[:, :], m8c[:, :], 0.0, None, ALU.not_equal).then_inc(keymask_set, 1)

                    def norm(step):
                        _, n, what = step
                        eps = LAYERS[n].eps
                        if what == "ctx":
                            dve.wait_ge(ctx_in, 32)
                        if what == "x":
                            dve.wait_ge(x_in, 16)
                        if what == "out":
                            dve.wait_ge(gamma_in, 32)
                        if what in ("mid", "out"):
                            wait_moved(dve, ("o", n, NT - 1))
                        src = cx if what == "ctx" else (v if (n, what) == (3, "mid") else x)
                        dst = x if what == "out" else zrow
                        for t in range(NT):
                            own(nc.vector.bn_stats(stats[:, t, :], src[:, t, :]))
                        for t in range(NT):
                            own(nc.vector.bn_aggr(mv[:, t, :], stats[:, t, :]))
                        if n == 3:
                            own(nc.vector.tensor_tensor(var[:, :], mv[:, :, 0], mv[:, :, 0], ALU.mult))
                            own(nc.vector.tensor_tensor(var[:, :], var[:, :], mv[:, :, 1], ALU.add))
                            nc.vector.tensor_scalar(var[:, :], var[:, :], eps, None, ALU.add).then_inc(var_done, 1)
                        else:
                            nc.vector.tensor_scalar(var[:, :], mv[:, :, 1], eps, None, ALU.add).then_inc(var_done, 1)
                        dve.wait_ge(rstd_done, N_NORM[step])
                        for t in range(NT):
                            if n == 3:
                                ins = nc.vector.tensor_scalar(dst[:, t, :], src[:, t, :], rstd[:, t:t + 1], None, ALU.mult)
                            else:
                                ins = nc.vector.tensor_scalar(dst[:, t, :], src[:, t, :], mv[:, t, 0:1], rstd[:, t:t + 1],
                                                              ALU.subtract, ALU.mult)
                            own(ins)
                            if n == 1:
                                own(nc.vector.tensor_tensor(x[:, t, :], x[:, t, :], row["gamma1"][:, :], ALU.mult))
                                own(nc.vector.tensor_tensor(x[:, t, :], x[:, t, :], row["beta1"][:, :], ALU.add))
                        dve.sem_inc(norm_done, 1)

                    for step in STEPS:
                        kind, n = step[0], step[1] if len(step) > 1 else None
                        L = LAYERS[n] if n in (0, 1, 2, 3) else None
                        if kind in RINGED:
                            bank = ring_bank(step)
                        if kind == "norm":
                            norm(step)
                        elif kind in ("ctxT", "maskT"):
                            wait_ring_full(dve, step)
                            dst = ctxT[:, step[1], :] if kind == "ctxT" else wide[:, 1, step[1], :]
                            nc.vector.tensor_copy(dst, bank[:, :]).then_inc(free_of(step), 1)
                        elif kind == "v":
                            t = step[2]
                            wait_ring_full(dve, step)
                            if n == 1:
                                ins = nc.vector.tensor_tensor(vone[:, t, :, 0:16],
                                                              bank[:, 0:128].rearrange("p (g d) -> p g d", g=8),
                                                              row["v1"][:, :].rearrange("p (g d) -> p g d", g=8), ALU.add)
                            elif n == 2:
                                ins = nc.vector.tensor_scalar(v[:, t, :], bank[:, :], mcolk[:, t:t + 1], None, ALU.mult)
                            else:
                                ins = nc.vector.tensor_tensor(v[:, t, :], bank[:, :], row[f"v{n}"][:, :], ALU.add)
                            ins.then_inc(free_of(step), 1)
                        elif kind in ("q", "k"):
                            u = step[2]
                            dve.wait_ge(hi_done, N_QK[step])
                            if n == 1:
                                if kind == "q":
                                    ins = nc.vector.tensor_tensor(q_lo, q_full[:, :], q_hi.bitcast(F32), ALU.subtract)
                                else:
                                    ins = nc.vector.scalar_tensor_tensor(out=k_lo, in0=bank[:, :], scalar=bias["k1"][:, 0:1],
                                                                         in1=k_hi.bitcast(F32), op0=ALU.add,
                                                                         op1=ALU.subtract)
                            else:
                                gb = unit_at(n, u) % UB
                                for j in range(4):
                                    src = bank[32 * j:32 * j + 32, :]
                                    if kind == "q":
                                        dst, hi = qs[32:64, gb, j, :], qs[0:32, gb, j, :]
                                    else:
                                        dst, hi = ks[64:96, gb, step[3], j, :], ks[0:32, gb, step[3], j, :]
                                    if n == 2:
                                        ins = nc.vector.tensor_tensor(dst, src, hi.bitcast(F32), ALU.subtract)
                                    else:
                                        ins = nc.vector.scalar_tensor_tensor(
                                            out=dst, in0=src, scalar=bias32[f"{kind}{n}"][:, 4 * u + j:4 * u + j + 1],
                                            in1=hi.bitcast(F32), op0=ALU.add, op1=ALU.subtract)
                            ins.then_inc(free_of(step), 1)
                        elif kind == "max":
                            u, j, t, h = step[2:]
                            g = unit_at(n, u)
                            wait_ring_full(dve, step)
                            col = mcol[:, g % 2, h, 4 * j + t:4 * j + t + 1]
                            if n == 1:
                                ins = nc.vector.tensor_tensor_reduce(bank[:, :], bank[:, :], wide[:, 0, t, :], 1.0, LOWEST,
                                                                     ALU.add, ALU.max, col)
                            else:
                                ins = nc.vector.tensor_reduce(col, bank[:, :], AX.X, ALU.max)
                            ins.then_inc(free_of(step), 1)
                            if L.halves == 2 and (j, t, h) == (3, NT - 1, 1):
                                wait_moved(dve, step)
                                nc.vector.tensor_tensor(mcol[:, g % 2, 0, :], mcol[:, g % 2, 0, :],
                                                        mcol[:, g % 2, 1, :], ALU.max).then_inc(max_done, 1)
                        elif kind == "maxT":
                            g = unit_at(n, step[2])
                            wait_ring_full(dve, step)
                            if g:
                                dve.wait_ge(mrow_in, 32 * g)
                            own(nc.vector.tensor_scalar(nm_hi[:, :], bank[0:16, 0:P], -1.0, None, ALU.mult))
                            nc.vector.scalar_tensor_tensor(out=nm_lo[:, :], in0=bank[0:16, 0:P], scalar=-1.0,
                                                           in1=nm_hi[:, :].bitcast(F32), op0=ALU.mult, op1=ALU.subtract
                                                           ).then_inc(free_of(step), 1)
                        elif kind == "score" and n == 1:
                            i, s = SINDEX[step], step[3]
                            dve.wait_ge(score_full, i + 1)
                            if i == SINDEX[("score", 1, 0, 0)]:
                                wait_moved(dve, ("maskT", NT - 1))
                            pair = s % 2
                            banks2 = score_banks[:, 2 * (i % 2):2 * (i % 2) + 2, :]
                            nc.vector.tensor_tensor(banks2, banks2, wide[:, 1, 2 * pair:2 * pair + 2, :], ALU.add
                                                    ).then_inc(score_masked, 1)
                        elif kind == "heads":
                            u = step[2]
                            g = unit_at(n, u)
                            dve.wait_ge(pv_done, last_pv(g))
                            before = sum(1 for m, _ in UNITS[:g] if m != 1)
                            if before:
                                dve.wait_ge(rden_done, before)
                            if n == 1:
                                if u:
                                    dve.wait_ge(heads1_moved, 128 * u)
                                ins = nc.vector.tensor_copy(heads1[:, :], num[:, :])
                                ins.then_inc(heads_done, 1)
                                dve.wait_ge(heads_done, u + 1)
                                dve.sem_inc(values_out, 1)
                                if u % 2:
                                    dve.wait_ge(heads1_moved, 128 * (u + 1))
                                    own(nc.vector.reciprocal(rden[:, :], rden[:, :]))
                                    nc.vector.tensor_tensor(at[:, u // 2, :], at[:, u // 2, :], rden[:, :], ALU.mult
                                                            ).then_inc(at_done, 1)
                            else:
                                nc.vector.transpose(denT[:, :], den[:, :]).then_inc(sums_out, 1)
                                dve.wait_ge(sums_out, before + 1)
                                own(nc.vector.reciprocal(denT[:, 0:S:32], denT[:, 0:S:32]))
                                if g:
                                    dve.wait_ge(at_done, at_count(g - 1))
                                nc.vector.transpose(rden[:, :], denT[:, 0:S:32].rearrange("p (a o) -> p a o", o=1
                                                                                          ).broadcast_to([P, S // 32, 32])
                                                    ).then_inc(rden_done, 1)
                        elif kind == "o":
                            t = step[2]
                            wait_ring_full(dve, step)
                            if n == 2:
                                ins = nc.vector.scalar_tensor_tensor(out=x[:, t, :], in0=bank[:, :], scalar=gtanh[:, 0:1],
                                                                     in1=x[:, t, :], op0=ALU.mult, op1=ALU.add)
                            else:
                                dst = v[:, t, :] if n == 3 else x[:, t, :]
                                own(nc.vector.tensor_tensor(bank[:, :], bank[:, :], row[f"o{n}"][:, :], ALU.add))
                                ins = nc.vector.tensor_tensor(dst, bank[:, :], x[:, t, :], ALU.add)
                            ins.then_inc(free_of(step), 1)
                        elif kind == "mlp_out":
                            dve.wait_ge(down_done, N_DOWN[("down", n, NFB - 1)])
                            for t in range(NT):
                                own(nc.vector.tensor_tensor(score_banks[:, t, :], score_banks[:, t, :], row[f"down{n}"][:, :], ALU.add))
                                own(nc.vector.tensor_tensor(x[:, t, :], score_banks[:, t, :], x[:, t, :], ALU.add))
                            dve.sem_inc(mlp_done, 1)
            for s in sems:
                nc.sync.sem_clear(s)
            nc.all_engine_barrier()


_F32 = ["x", "ctx_2048", "mask_Bx1xSxS2_ff0"]
_VECS = ["L0_xattn_ln1_w", "L0_xattn_ln1_b", "L0_xattn_q_b", "L0_xattn_k_b", "L0_xattn_v_b", "L0_xattn_cproj_b",
         "L0_xattn_ln2_w", "L0_xattn_ln2_b", "L0_xattn_fc_b", "L0_xattn_proj_b", "L1_xattn_bq", "L1_xattn_bk",
         "L1_xattn_bv", "L1_xattn_bo", "L1_xattn_gamma", "L1_xattn_beta", "L2_xattn_ln_gamma",
         "L2_xattn_ln_beta", "L2_xattn_gate", "L3_xattn_q_b", "L3_xattn_out_b", "L3_xattn_postnorm_w",
         "L3_xattn_mlp_b1", "L3_xattn_mlp_b2"]
_BY_HEAD = ["L0_xattn_q_b", "L0_xattn_k_b", "L3_xattn_q_b", "L3_k_b"]
_BY_PARTITION = ["L1_xattn_bq", "L1_xattn_bk",
                 "L0_xattn_ln1_w", "L0_xattn_ln1_b", "L0_xattn_ln2_w", "L0_xattn_ln2_b", "L2_xattn_ln_gamma",
                 "L2_xattn_ln_beta", "L3_xattn_postnorm_w", "L0_xattn_fc_b", "L3_xattn_mlp_b1"]
_WEIGHTS = {"q0": "L0_xattn_q_w", "k0": "L0_xattn_k_w", "v0": "L0_xattn_v_w", "o0": "L0_xattn_cproj_w",
            "up0": "L0_xattn_fc_w", "down0": "L0_xattn_proj_w", "q1": "L1_xattn_Wq", "k1": "L1_xattn_Wk",
            "v1": "L1_xattn_Wv", "o1": "L1_xattn_Wo", "q3": "L3_xattn_q_w", "o3": "L3_xattn_out_w",
            "up3": "L3_xattn_mlp_w1", "down3": "L3_xattn_mlp_w2"}


def kernel(**inputs):
    import numpy as np
    import concourse.bacc as bacc
    from concourse.bass_utils import run_bass_kernel_spmd as run

    a = {k: np.ascontiguousarray(inputs[k]) for k in _F32 + _VECS + ["mask_BxS2_ik0"]}
    a["mask8"] = np.ascontiguousarray(inputs["mask_BxS2_bf1"]).view(np.uint8)
    a["mask8_cols"] = np.ascontiguousarray(a["mask8"].reshape(B, NT, P).transpose(0, 2, 1))
    for k, name in _WEIGHTS.items():
        a[k] = np.ascontiguousarray(inputs[name])
    for k, name in (("q2", "L2_xattn_Wq"), ("k2", "L2_xattn_Wk"), ("v2", "L2_xattn_Wv"), ("o2", "L2_xattn_Wo")):
        a[k] = np.ascontiguousarray(np.asarray(inputs[name]).T)
    kv_w, kv_b = np.asarray(inputs["L3_xattn_kv_w"]), np.asarray(inputs["L3_xattn_kv_b"])
    a["k3"], a["v3"] = np.ascontiguousarray(kv_w[:, 0::2]), np.ascontiguousarray(kv_w[:, 1::2])
    a["L3_k_b"], a["L3_v_b"] = np.ascontiguousarray(kv_b[0::2]), np.ascontiguousarray(kv_b[1::2])

    for k in _BY_HEAD:
        a[k] = np.ascontiguousarray(a[k].reshape(-1, 32).T)
    for k in _BY_PARTITION:
        a[k] = np.ascontiguousarray(a[k].reshape(-1, P).T)

    nc = bacc.Bacc("TRN2", target_bir_lowering=False, num_devices=1)
    arrays, args = {}, {}
    for k, arr in a.items():
        arrays[f"in_{k}"] = arr
        args[k] = nc.dram_tensor(f"in_{k}", arr.shape, mybir.dt.from_np(arr.dtype), kind="ExternalInput").ap()
    out = nc.dram_tensor("out_0", (B, S, D), F32, kind="ExternalOutput").ap()
    build(nc, args, out)
    r = run(nc, [arrays], core_ids=[0])
    return r.results[0]["out_0"]
```

```python
from contextlib import ExitStack

import numpy as np

import concourse.bass as bass
from concourse import mybir

ALU = mybir.AluOpType
ACT = mybir.ActivationFunctionType
AX = mybir.AxisListType
F32 = mybir.dt.float32
F32R = mybir.dt.float32r
U8 = mybir.dt.uint8
I32 = mybir.dt.int32

P = 128
B, S, D = 4, 512, 512
NT = S // P
NC = D // P
NFB = 4
MASKED = -(2.0 ** 100)
LOWEST = float(np.finfo(np.float32).min)
WSLOTS = 3
UB = 3
PTB = 3
RING = 2


class Layer:
    def __init__(self, n, hd, units, keys, scale, eps, vcols):
        self.n, self.hd, self.units, self.keys, self.scale, self.eps = n, hd, units, keys, scale, eps
        self.copies = 3 if hd == 32 else 4
        self.row = self.copies * hd
        self.kt = keys // P
        self.halves = keys // S
        self.slots = 4 * self.kt // 2
        self.kheads = 4 if hd == 32 else 1
        self.vcols = vcols


LAYERS = [
    Layer(0, 32, 4, 512, 32 ** -0.5, 1e-5, 512),
    Layer(1, 16, 8, 512, 1.0, 1e-6, 128),
    Layer(2, 32, 4, 512, 32 ** -0.5, 1e-5, 512),
    Layer(3, 32, 4, 1024, 1.0 / 32, 1e-6, 512),
]
UNITS = [(L.n, u) for L in LAYERS for u in range(L.units)]

WEIGHTS = []
for _n in range(4):
    WEIGHTS += [(_n, w) for w in (("k", "v", "q", "o") if _n == 1 else ("v", "q", "k", "o"))]
    if _n in (0, 3):
        WEIGHTS += [(_n, "up0")] + [(_n, w) for f in range(1, NFB) for w in (f"up{f}", f"down{f - 1}")]
        WEIGHTS += [(_n, f"down{NFB - 1}")]
WINDEX = {w: i for i, w in enumerate(WEIGHTS)}


def gqa_heads(L):
    def scores(h):
        return [("max", 1, h // 4, h % 4, t, 0) for t in range(NT)] if h < 4 * L.units else []

    steps, waiting = scores(0), ([], [])
    for h in range(4 * L.units):
        (u, j), ahead = divmod(h, 4), scores(h + 1)
        steps += ahead[0:1] + waiting[0] + ahead[1:2] + [("score", 1, u, 2 * j)] + ahead[2:3] + waiting[1]
        if u % 2 == 0 and j == 1 and u + 2 < L.units:
            steps.append(("q", 1, u // 2 + 1))
        steps += ahead[3:] + [("score", 1, u, 2 * j + 1)]
        waiting = [("pv", 1, u, 2 * j)], [("pv", 1, u, 2 * j + 1)] + ([("heads", 1, u)] if j == 3 else [])
    return steps + waiting[0] + waiting[1]


def layer_steps(L):
    n = L.n

    def project(u):
        return [("q", n, u)] + [("k", n, u, h) for h in range(L.halves)]

    def maxima(u):
        return [("max", n, u, j, t, h) for j in range(4) for t in range(NT) for h in range(L.halves)] + [("maxT", n, u)]

    def mix(main, extra):
        out, done = [], 0
        for i, step in enumerate(main):
            upto = len(extra) * (i + 1) // len(main)
            out += [step] + extra[done:upto]
            done = upto
        return out

    values = [("v", n, t) for t in range(L.kt)]
    if n == 0:
        steps = [("ctxT", c) for c in range(NC)] + [("norm", 0, "x")] + values[0:2]
        steps += [("xT", 0, "z", c) for c in range(NC)] + project(0) + values[2:3]
        later = values[3:] + project(1) + project(2)
        steps += mix(later[:-1], maxima(0)) + later[-1:]
    elif n == 1:
        steps = [("k", 1, 0, 0)] + [("xT", 1, "x", c) for c in range(NC)] + [("q", 1, 0)] + values
        steps += gqa_heads(L)
    elif n == 2:
        steps = [("aT", c) for c in range(NC)] + [("norm", 1, "out")] + values[0:3]
        steps += [("xT", 2, "x", c) for c in range(NC)] + project(0) + values[3:]
        later = project(1) + project(2)
        steps += mix(later[:-1], maxima(0)) + later[-1:]
    else:
        steps = [("xT", 3, "x", c) for c in range(NC)] + project(0) + values[0:1]
        later = values[1:] + project(1) + project(2)
        steps += mix(later[:-2], maxima(0)) + later[-2:]
    for u in range(L.units if n != 1 else 0):
        fill = (project(u + 2) if 1 <= u < L.units - 2 else [])
        fill += (maxima(u + 1) if u + 1 < L.units else [])
        done = 0
        steps.append(("score", n, u, 0))
        for s in range(L.slots):
            upto = min(len(fill) * (s + 1) // (L.slots - 3), len(fill))
            part = fill[done:upto]
            steps += part[0:1]
            if s + 1 < L.slots:
                steps.append(("score", n, u, s + 1))
            steps += part[1:2] + [("pv_half", n, u, s)] + part[2:3] + [("pv", n, u, s)] + part[3:]
            done = upto
        steps += [("heads", n, u)]
    steps += [("o", n, t) for t in range(NT)]
    if n in (0, 3):
        steps += [("norm", n, "mid")] + [("xT", n, "mid", c) for c in range(NC)]
        if n == 0:
            steps.append(("ctx_in",))
        for f in range(NFB):
            steps += [("up", n, f, m) for m in range(NC)]
            if f:
                steps.append(("down", n, f - 1))
            if n == 0 and f == 1:
                steps.append(("norm", 2, "ctx"))
        if n == 0:
            steps.append(("mask_in",))
        steps += [("down", n, NFB - 1), ("mlp_out", n)]
    return steps


STEPS = [s for L in LAYERS for s in layer_steps(L)]
RINGED = ("ctxT", "xT", "aT", "v", "q", "k", "max", "maxT", "o", "up")
RING_STEPS = [s for s in STEPS if s[0] in RINGED]
RINDEX = {s: i for i, s in enumerate(RING_STEPS)}
SCORE_STEPS = [s for s in STEPS if s[0] == "score"]
SINDEX = {s: i for i, s in enumerate(SCORE_STEPS)}
BY_VECTOR = [s[1] == 1 and s[3] in (1, 4, 7) for s in SCORE_STEPS]


def last_use():
    out = {}
    for i, (n, name) in enumerate(WEIGHTS):
        if name[:2] == "up":
            out["up", n, int(name[2:]), NC - 1] = i
        elif name[:4] == "down":
            out["down", n, int(name[4:])] = i
        else:
            out[[s for s in STEPS if s[:2] == (name, n)][-1]] = i
    return out


LAST_USE = last_use()


def order(kinds):
    return {s: i + 1 for i, s in enumerate([s for s in STEPS if s[0] in kinds])}


def build(nc, A, out):
    ctx = ExitStack()

    def sb(name, shape, dt=F32):
        return ctx.enter_context(nc.sbuf_tensor(name, shape, dt))

    def sem(name):
        s = ctx.enter_context(nc.semaphore(name))
        sems.append(s)
        return s

    with ctx:
        sems = []
        w = sb("w", [P, WSLOTS, NC, D])
        x = sb("x", [P, NT, D])
        ctxT = sb("ctxT", [P, NC, S])
        xT = sb("xT", [P, NC, S])
        at = sb("at", [P, NC, S])
        v = sb("v", [P, 8, D])
        cx = v[:, 0:NT, :]
        wide = sb("wide", [P, 2, NC, D])
        pq = [wide[:, 1], v[:, NT:2 * NT, :]]
        qs = sb("qs", [P, UB, 4, S], F32R)
        ks = sb("ks", [P, UB, 2, 4, S], F32R)
        ks1 = ks[:, 0]
        qs1 = [ks[:, 1], ks[:, 2], qs[:, 0:2]]
        parts = {kind: (sb(f"{kind}_full", [P, S]), sb(f"{kind}_high", [P, S])) for kind in ("q", "k")}
        pt = sb("pt", [P, PTB, 2, S])
        rden = sb("rden", [P, S])
        denT = sb("denT", [P, S])
        rec1 = sb("rec1", [P, S // 32, 2])
        lanes = sb("lanes", [P, 2])
        vone = sb("vone", [P, NT, 4, 64])
        mcol = sb("mcol", [P, 2, 2, 16])
        nm_hi = sb("nm_hi", [16, P], F32R)
        nm_lo = sb("nm_lo", [16, P], F32R)
        m8 = sb("m8", [1, S], U8)
        m32, mtmp = pt[0:1, 0, 0, :].bitcast(I32), pt[0:1, 0, 1, :]
        krow = [pt[0:1, 1, i, :] for i in range(2)]
        stash = qs[100:101, 0, 0, :]
        mcolk = sb("mcolk", [P, NT])
        m8c = sb("m8c", [P, NT], U8)
        ones = sb("ones", [P, 32])
        ident = sb("ident", [P, P])
        stats = sb("stats", [P, NT, 6])
        mv = sb("mv", [P, NT, 2])
        rstd = sb("rstd", [P, NT])
        var = sb("var", [P, NT])
        minus_half = sb("minus_half", [P, NT])
        gate = sb("gate", [P, 1])
        gtanh = sb("gtanh", [P, 1])
        bias = {k: sb(f"c_{k}", [P, NC]) for k in
                ("q0", "k0", "q3", "k3", "q1", "w10", "b10", "w20", "b20", "w2", "b2", "w3")}
        bias["k1"] = sb("c_k1", [P, 1])
        bq4 = sb("bq4", [P, NC])
        bup = {0: sb("c_up0", [P, NFB * NC]), 3: sb("c_up3", [P, NFB * NC])}
        row = {k: sb(f"r_{k}", [P, D]) for k in
               ("v0", "o0", "down0", "o1", "v3", "o3", "down3")}
        row["gamma1"], row["beta1"] = pt[:, 0, 0, :], pt[:, 0, 1, :]
        row["v1"] = sb("r_v1", [P, 128])

        banks = [ctx.enter_context(nc.psum_tensor(f"bank{i}", [P, 512], F32)) for i in range(4, 8)]
        score_banks = ctx.enter_context(nc.psum_tensor("score_banks", [P, 4, 512], F32))
        ring = banks[0:2]
        num, den = banks[2], banks[3]

        const_in = ctx.enter_context(nc.semaphore("const_in"))
        const_set = ctx.enter_context(nc.semaphore("const_set"))
        gate_set = ctx.enter_context(nc.semaphore("gate_set"))
        x_in, ctx_in, mask_in, out_stored = sem("x_in"), sem("ctx_in"), sem("mask_in"), sem("out_stored")
        keymask_in = sem("keymask_in")
        keymask_set = sem("keymask_set")
        w_in = [sem(f"w_in{i}") for i in range(WSLOTS)]
        ring_full = sem("ring_full")
        ring_free = [sem(f"ring_free{i}") for i in range(RING)]
        by_vector = sem("by_vector")
        norm_done = sem("norm_done")
        var_done, rstd_done = sem("var_done"), sem("rstd_done")
        hi_done, lo_done = sem("hi_done"), sem("lo_done")
        split_stacked = {"q": sem("q_stacked"), "k": sem("k_stacked")}
        krows_in, rows1_in = sem("krows_in"), sem("rows1_in")
        krow3_in = [sem(f"krow3_in{i}") for i in range(UB)]
        values1_out, joined = sem("values1_out"), sem("joined")
        sums_out, values_out = sem("sums_out"), sem("values_out")
        rden_done, at_done = sem("rden_done"), sem("at_done")
        gamma_in = sem("gamma_in")
        max_done = sem("max_done")
        mrow_in = sem("mrow_in")
        score_full = sem("score_full")
        mask_negated = sem("mask_negated")
        exp1_done = sem("exp1_done")
        copied = sem("copied")
        exp_done, pv_done = sem("exp_done"), sem("pv_done")
        down_done = sem("down_done")
        mlp_done = sem("mlp_done")

        N_NORM = order(("norm",))
        N_QK = order(("q", "k"))
        N_PV = order(("pv",))
        N_MLP = {s: NT * i for s, i in order(("mlp_out",)).items()}
        N_DOWN, downs = {}, 0
        for s in STEPS:
            if s[0] == "down":
                downs += NT if s[2] == NFB - 1 else 1
                N_DOWN[s] = downs
        N_MAX1 = {s: i + 1 for i, s in enumerate([s for s in STEPS if s[0] == "max" and s[1] == 1])}

        def probs_sem(i):
            return (copied if BY_VECTOR[i] else exp_done), BY_VECTOR[:i + 1].count(BY_VECTOR[i])

        def wait_probs(eng, i):
            which, count = probs_sem(i)
            eng.wait_ge(which, count)

        def unit_at(n, u):
            return UNITS.index((n, u))

        def stack_count(kind, n, u, h):
            steps = [s for s in STEPS if s[0] == kind]
            here = steps.index((kind, n, u) if kind == "q" else (kind, n, u, h))
            return 16 * sum(LAYERS[s[1]].copies for s in steps[:here + 1])

        def wait_stacked(eng, g):
            n, u = UNITS[g]
            eng.wait_ge(split_stacked["q"], stack_count("q", n, u // 2 if n == 1 else u, 0))
            eng.wait_ge(split_stacked["k"], stack_count("k", n, 0 if n == 1 else u, LAYERS[n].halves - 1))
            if n == 0:
                eng.wait_ge(krows_in, 16 * (UB + 1))
            elif n == 1:
                eng.wait_ge(rows1_in, 64)
            elif n == 3:
                eng.wait_ge(krow3_in[g % UB], 16)

        def last_pv(g):
            n, u = UNITS[g]
            return N_PV[("pv", n, u, LAYERS[n].slots - 1)]

        def at_count(g):
            return sum(1 for n, u in UNITS[:g + 1] if n != 1 or u % 2)

        def values_count(g):
            return sum(1 for n, _ in UNITS[:g + 1] if n != 1)

        def q_of(g):
            n, u = UNITS[g]
            return qs1[u // 2 % 3][:, u % 2] if n == 1 else qs[:, g % UB]

        def k_of(g, half, head):
            n, u = UNITS[g]
            return ks1[:, u // 4, u % 4] if n == 1 else ks[:, g % UB, half, head]

        def wait_unit_buffers(eng, g):
            n, u = UNITS[g]
            if n == 1 and u >= 6:
                eng.wait_ge(pv_done, last_pv(unit_at(1, 1)))
            elif n == 1:
                eng.wait_ge(pv_done, last_pv(unit_at(0, 3)))
            elif UNITS[g][0] == 2 and UNITS[g][1] < UB:
                eng.wait_ge(pv_done, last_pv(unit_at(1, 7)))
            elif g >= UB:
                eng.wait_ge(pv_done, last_pv(g - UB))

        def ring_bank(step):
            return ring[RINDEX[step] % RING]

        def wait_ring_full(eng, step):
            eng.wait_ge(ring_full, RINDEX[step] + 1)

        def free_of(step):
            return ring_free[RINDEX[step] % RING]

        def wait_moved(eng, step):
            for i in range(max(RINDEX[step] - RING + 1, 0), RINDEX[step] + 1):
                eng.wait_ge(ring_free[i % RING], i // RING + 1)

        def wait_weights_used(eng, n, name):
            step = [s for s, i in LAST_USE.items() if WEIGHTS[i] == (n, name)][0]
            if step[0] == "down":
                eng.wait_ge(down_done, N_DOWN[step])
            else:
                wait_ring_full(eng, step)

        def w_ap(n, name):
            return w[:, WINDEX[(n, name)] % WSLOTS]

        def bcast(ap, cols):
            return ap.rearrange("(o n) -> o n", o=1).broadcast_to([P, cols])

        zrow = at

        CONSTS = []
        for key, name in (("q0", "L0_xattn_q_b"), ("k0", "L0_xattn_k_b"), ("q3", "L3_xattn_q_b"), ("k3", "L3_k_b"),
                          ("q1", "L1_xattn_bq"), ("k1", "L1_xattn_bk"), ("w10", "L0_xattn_ln1_w"),
                          ("b10", "L0_xattn_ln1_b"), ("w20", "L0_xattn_ln2_w"), ("b20", "L0_xattn_ln2_b"),
                          ("w2", "L2_xattn_ln_gamma"), ("b2", "L2_xattn_ln_beta"), ("w3", "L3_xattn_postnorm_w")):
            CONSTS.append((bias[key][:, :], A[name]))
        CONSTS.append((bup[0][:, :], A["L0_xattn_fc_b"]))
        CONSTS.append((bup[3][:, :], A["L3_xattn_mlp_b1"]))
        for key, name in (("v0", "L0_xattn_v_b"), ("o0", "L0_xattn_cproj_b"), ("down0", "L0_xattn_proj_b"),
                          ("v1", "L1_xattn_bv"), ("o1", "L1_xattn_bo"), ("v3", "L3_v_b"), ("o3", "L3_xattn_out_b"),
                          ("down3", "L3_xattn_mlp_b2")):
            CONSTS.append((row[key][:, :], bcast(A[name], row[key].shape[1])))
        CONSTS.append((lanes[:, :], A["lanes"]))
        CONSTS.append((gate[:, :], bcast(A["L2_xattn_gate"], 1)))

        with nc.Block() as block:
            @block.sync
            def _(sp):
                for dst, src in CONSTS:
                    sp.dma_start(dst, src, allow_slow_non_contiguous=True).then_inc(const_in, 16)

            @block.gpsimd
            def _(pool):
                nc.gpsimd.memset(ident[:, :], 0.0).then_inc(const_set, 1)
                nc.gpsimd.memset(ones[:, :], 1.0).then_inc(const_set, 1)
                pool.wait_ge(const_set, 2)
                nc.gpsimd.memset(qs[96:128].bitcast(F32), 1.0).then_inc(const_set, 1)
                pool.wait_ge(const_set, 3)
                nc.gpsimd.memset(ks[96:128].bitcast(F32), 1.0).then_inc(const_set, 1)
                pool.wait_ge(const_set, 4)
                nc.gpsimd.memset(vone[:, :, :, :], 1.0).then_inc(const_set, 1)
                nc.gpsimd.memset(minus_half[:, :], -0.5).then_inc(const_set, 1)
                pool.wait_ge(const_set, 6)
                nc.gpsimd.affine_select(out=ident[:, :], in_=ident[:, :], compare_op=ALU.not_equal, fill=1.0,
                                        base=0, pattern=[[-1, P]], channel_multiplier=1).then_inc(const_set, 1)
                pool.wait_ge(const_set, 7)
                nc.gpsimd.memset(ks[96:97, :, 1].bitcast(F32), 0.0).then_inc(const_set, 1)

            @block.scalar
            def _(act):
                act.wait_ge(const_in, 16 * len(CONSTS))
                nc.scalar.activation(gtanh[:, :], gate[:, :], ACT.Tanh).then_inc(gate_set, 1)
                nc.scalar.activation(bq4[:, :], bias["q1"][:, :], ACT.Copy, scale=-0.25).then_inc(gate_set, 1)

            @block.vector
            def _(dve):
                dve.wait_ge(const_in, 16 * len(CONSTS))
                dve.wait_ge(const_set, 8)
                dve.wait_ge(gate_set, 2)

        with nc.Fori(0, B) as b:
            block = nc.Block()
            with block:
                @block.sync
                def _(sp):
                    def tokens(ap):
                        return ap[bass.ds(b, 1)].rearrange("o (t p) d -> p (o t) d", p=P)

                    def load_weights(i):
                        n, name = WEIGHTS[i]
                        if i >= WSLOTS:
                            wait_weights_used(sp, *WEIGHTS[i - WSLOTS])
                        if name[:2] == "up":
                            f = int(name[2:])
                            src = A[f"up{n}"][:, f * D:(f + 1) * D]
                        elif name[:4] == "down":
                            f = int(name[4:])
                            src = A[f"down{n}"][f * D:(f + 1) * D, :]
                        else:
                            src = A[f"{name}{n}"]
                        sp.dma_start(w[:, i % WSLOTS, :, 0:src.shape[1]], src.rearrange("(c p) n -> p c n", p=P)
                                       ).then_inc(w_in[i % WSLOTS], 16)

                    sp.dma_start(cx, tokens(A["ctx_2048"])).then_inc(ctx_in, 16)
                    sp.dma_start(x[:, :, :], tokens(A["x"])).then_inc(x_in, 16)
                    sp.dma_start(m8[:, :], A["mask8"][bass.ds(b, 1), :]).then_inc(keymask_in, 16)
                    sp.dma_start(m32, A["mask_BxS2_ik0"][bass.ds(b, 1), :]).then_inc(keymask_in, 16)
                    sp.dma_start(m8c[:, :], A["mask8_cols"][bass.ds(b, 1)].rearrange("o p t -> p (o t)")
                                 ).then_inc(keymask_in, 16)
                    for i in range(WSLOTS):
                        load_weights(i)
                    sp.wait_ge(keymask_set, 1)
                    for i in range(UB):
                        sp.dma_start(ks[96:97, i, 0].bitcast(F32), krow[0].rearrange("p (o s) -> p o s", o=1).broadcast_to([1, 4, S])
                                     ).then_inc(krows_in, 16)
                    sp.dma_start(stash.bitcast(F32), krow[1]).then_inc(krows_in, 16)
                    for step in STEPS:
                        kind, n = step[0], step[1] if len(step) > 1 else None
                        if kind == "ctx_in":
                            sp.wait_ge(pv_done, last_pv(unit_at(0, 3)))
                            sp.dma_start(cx, tokens(A["ctx_2048"])).then_inc(ctx_in, 16)
                            row1 = LAYERS[1].row
                            sp.dma_start(ks1[row1:row1 + 3].bitcast(F32).rearrange("p a b s -> p (a b) s"),
                                         ks[96:99, 0, 1, 0:1, :].bitcast(F32).broadcast_to([3, 8, S])).then_inc(rows1_in, 16)
                            for pair in qs1:
                                sp.dma_start(pair[row1:row1 + 1].bitcast(F32).rearrange("p a b s -> p (a b) s"),
                                             qs[96:97, 0, 0:1, :].bitcast(F32).broadcast_to([1, 8, S])).then_inc(rows1_in, 16)
                        elif kind == "mask_in":
                            sp.wait_ge(down_done, N_DOWN[("down", 0, NFB - 2)])
                            sp.dma_start(wide[:, 0], A["mask_Bx1xSxS2_ff0"][bass.ds(b, 1)].rearrange(
                                "o a (t p) k -> p (o a t) k", p=P)).then_inc(mask_in, 16)
                        elif kind in ("q", "k"):
                            u, L = step[2], LAYERS[n]
                            g = unit_at(n, 2 * u) if (kind, n) == ("q", 1) else unit_at(n, u)
                            hd = L.hd
                            wait_unit_buffers(sp, g)
                            if kind == "k" and n == 3 and u < UB and step[3] == 0:
                                sp.dma_start(ks[96:97, g % UB, 0].bitcast(F32), stash.bitcast(F32).rearrange(
                                    "p (o s) -> p o s", o=1).broadcast_to([1, 4, S])).then_inc(krow3_in[g % UB], 16)
                            if n != 1:
                                stack = qs[:, g % UB] if kind == "q" else ks[:, g % UB, step[3]]
                            elif kind == "q":
                                stack = qs1[u % 3].rearrange("p a b s -> p (a b) s")
                            else:
                                stack = ks1.rearrange("p a b s -> p (a b) s")
                            low, high = parts[kind]
                            stacking = (high, low, high, low) if kind == "q" else (high, high, low, low)
                            if n != 1 and kind == "k":
                                stacking = (high, high, low)
                            sp.wait_ge(lo_done, N_QK[step])
                            for i in range(L.copies):
                                sp.dma_start(stack[hd * i:hd * (i + 1)].bitcast(F32), stacking[i][:, :]
                                             ).then_inc(split_stacked[kind], 16)
                        elif kind == "maxT":
                            u, L = step[2], LAYERS[n]
                            g = unit_at(n, u)
                            wait_moved(sp, step)
                            for i, part in enumerate((nm_hi, nm_lo)):
                                sp.dma_start(q_of(g)[L.row + 1 + i:L.row + 2 + i].bitcast(F32).rearrange(
                                    "o j (t n) -> o (j t) n", n=P), part[:, :].bitcast(F32)).then_inc(mrow_in, 16)
                        elif kind == "heads" and n == 1:
                            u = step[2]
                            if u == LAYERS[1].units - 1:
                                sp.wait_ge(pv_done, last_pv(unit_at(1, u)))
                                sp.dma_start(row["gamma1"], bcast(A["L1_xattn_gamma"], D)).then_inc(gamma_in, 16)
                                sp.dma_start(row["beta1"], bcast(A["L1_xattn_beta"], D)).then_inc(gamma_in, 16)
                        if step in LAST_USE and LAST_USE[step] + WSLOTS < len(WEIGHTS):
                            load_weights(LAST_USE[step] + WSLOTS)
                    for t in range(NT):
                        sp.wait_ge(mlp_done, N_MLP[("mlp_out", 3)] - (NT - 1 - t))
                        sp.dma_start(out[bass.ds(b, 1), t * P:(t + 1) * P].rearrange("o p d -> p (o d)"), x[:, t, :]
                                     ).then_inc(out_stored, 16)
                    sp.wait_ge(out_stored, 16 * NT)

                @block.gpsimd
                def _(pool):
                    for step in STEPS:
                        if step[0] == "norm":
                            pool.wait_ge(var_done, N_NORM[step])
                            nc.gpsimd.tensor_tensor(rstd[:, :], var[:, :], minus_half[:, :], ALU.pow
                                                    ).then_inc(rstd_done, 1)
                        elif step[0] == "mask_in":
                            pool.wait_ge(mask_in, 16)
                            nc.gpsimd.tensor_scalar(wide[:, 0], wide[:, 0], -1.0, None, ALU.mult).then_inc(mask_negated, 1)
                        elif step[0] in ("q", "k"):
                            full, high = parts[step[0]]
                            pool.wait_ge(hi_done, N_QK[step])
                            nc.gpsimd.tensor_tensor(full[:, :].bitcast(F32R), full[:, :], high[:, :], ALU.subtract
                                                    ).then_inc(lo_done, 1)
                        elif step[0] == "heads" and (step[1] != 1 or step[2] % 2):
                            _, n, u = step
                            g = unit_at(n, u)
                            if n == 1:
                                pool.wait_ge(joined, (u + 1) // 2)
                                c = u // 2
                            else:
                                pool.wait_ge(values_out, values_count(g))
                                c = u
                            pool.wait_ge(rden_done, at_count(g))
                            nc.gpsimd.tensor_tensor(at[:, c, :], at[:, c, :], rden[:, :], ALU.mult).then_inc(at_done, 1)

                @block.tensor
                def _(pe):
                    landed = [0]

                    def need_weight(n, name):
                        i = WINDEX[(n, name)]
                        while landed[0] <= i:
                            k = landed[0]
                            pe.wait_ge(w_in[k % WSLOTS], 16 * (k // WSLOTS + 1))
                            landed[0] += 1

                    def take_ring(step):
                        i = RINDEX[step]
                        if i >= RING:
                            pe.wait_ge(ring_free[i % RING], i // RING)
                        return ring[i % RING]

                    def project_T(step, n, name, cols, src, c0=0):
                        o = take_ring(step)
                        wt = w_ap(n, name)
                        for c in range(NC):
                            last = nc.tensor.matmul(o[:, :], wt[:, c, cols[0]:cols[1]], src[:, c, :],
                                                    start=(c == 0), stop=(c == NC - 1))
                        return last

                    for step in STEPS:
                        kind, n = step[0], step[1] if len(step) > 1 else None
                        L = LAYERS[n] if n in (0, 1, 2, 3) else None
                        if kind in ("ctxT", "xT", "aT"):
                            if kind == "ctxT":
                                pe.wait_ge(ctx_in, 16)
                                src, c = cx, step[1]
                            elif kind == "xT":
                                src, c = {"x": x, "z": zrow, "mid": zrow}[step[2]], step[3]
                                if step[2] == "z":
                                    pe.wait_ge(norm_done, N_NORM[("norm", 0, "x")])
                                elif step[2] == "mid":
                                    pe.wait_ge(norm_done, N_NORM[("norm", n, "mid")])
                                elif n == 1:
                                    pass
                                elif n == 2:
                                    pe.wait_ge(norm_done, N_NORM[("norm", 1, "out")])
                                else:
                                    wait_moved(pe, ("o", 2, NT - 1))
                            elif kind == "aT":
                                pe.wait_ge(norm_done, N_NORM[("norm", 2, "ctx")])
                                src, c = cx, step[1]
                            o = take_ring(step)
                            for t in range(NT):
                                if step == ("xT", 1, "x", 0):
                                    pe.wait_ge(mlp_done, N_MLP[("mlp_out", 0)] - (NT - 1 - t))
                                last = nc.tensor.transpose(o[:, t * P:(t + 1) * P], src[:, t, c * P:(c + 1) * P], ident[:, :])
                            last.then_inc(ring_full, 1)
                        elif kind == "v":
                            t = step[2]
                            need_weight(n, "v")
                            if n == 2:
                                wait_moved(pe, ("aT", NC - 1))
                                src, t0 = wide[:, 0], t
                            elif t < NT:
                                wait_moved(pe, ("ctxT", NC - 1))
                                src, t0 = ctxT, t
                            else:
                                wait_moved(pe, ("xT", 3, "x", NC - 1))
                                src, t0 = xT, t - NT
                            o = take_ring(step)
                            wt = w_ap(n, "v")
                            for c in range(NC):
                                last = nc.tensor.matmul(o[:, 0:L.vcols], src[:, c, t0 * P:(t0 + 1) * P], wt[:, c, 0:L.vcols],
                                                        start=(c == 0), stop=(c == NC - 1))
                            last.then_inc(ring_full, 1)
                        elif kind in ("q", "k"):
                            u = step[2]
                            need_weight(n, kind)
                            if kind == "q":
                                wait_moved(pe, ("xT", n, "z" if n == 0 else "x", NC - 1))
                                src = xT
                            else:
                                if n == 2:
                                    src = wide[:, 0]
                                elif step[3] == 1:
                                    src = xT
                                else:
                                    src = ctxT
                            last = project_T(step, n, kind, (u * P, (u + 1) * P), src)
                            last.then_inc(ring_full, 1)
                        elif kind == "max":
                            u, j, t, h = step[2:]
                            g = unit_at(n, u)
                            wait_stacked(pe, g)
                            o = take_ring(step)
                            kh = j if L.kheads == 4 else 0
                            nc.tensor.matmul(o[:, :], q_of(g)[0:L.row + 1, j, t * P:(t + 1) * P],
                                             k_of(g, h, kh)[0:L.row + 1, :],
                                             start=True, stop=True).then_inc(ring_full, 1)
                        elif kind == "maxT":
                            g = unit_at(n, step[2])
                            if L.halves == 2:
                                pe.wait_ge(max_done, step[2] + 1)
                            else:
                                wait_moved(pe, ("max", n, step[2], 3, NT - 1, 0))
                            o = take_ring(step)
                            nc.tensor.transpose(o[0:16, 0:P], mcol[:, g % 2, 0, :], ident[:, :]).then_inc(ring_full, 1)
                        elif kind == "score":
                            u, s = step[2:]
                            g, i = unit_at(n, u), SINDEX[step]
                            if s == 0 and n != 1:
                                pe.wait_ge(mrow_in, 32 * values_count(g))
                            if i >= 2:
                                wait_probs(pe, i - 2)
                            if n == 1:
                                j = s // 2
                                pe.wait_ge(exp1_done, N_MAX1[("max", 1, u, j, NT - 1, 0)])
                                for a in range(2):
                                    kt = s % 2 * 2 + a
                                    for t in range(NT):
                                        last = nc.tensor.transpose(score_banks[:, 2 * (i % 2) + a, t * P:(t + 1) * P],
                                                                   pq[j % 2][:, t, kt * P:(kt + 1) * P], ident[:, :])
                                last.then_inc(score_full, 1)
                                continue
                            j, pair = s // (L.kt // 2), s % (L.kt // 2)
                            kh = j if L.kheads == 4 else 0
                            for a in range(2):
                                kt = 2 * pair + a
                                last = nc.tensor.matmul(score_banks[:, 2 * (i % 2) + a, :],
                                                        k_of(g, kt // NT, kh)[0:L.row + 3, kt % NT * P:(kt % NT + 1) * P],
                                                        q_of(g)[0:L.row + 3, j, :], start=True, stop=True)
                            last.then_inc(score_full, 1)
                        elif kind in ("pv_half", "pv"):
                            u, s = step[2:]
                            tiles = (0, 1) if n == 1 else (0,) if kind == "pv_half" else (1,)
                            g, i = unit_at(n, u), SINDEX[("score", n, u, s)]
                            if s == 0 and 0 in tiles:
                                wait_moved(pe, ("v", n, L.kt - 1))
                                if n == 1 and u >= 2:
                                    pe.wait_ge(sums_out, g - 1)
                                    pe.wait_ge(joined if u % 2 else values1_out, u // 2)
                                elif g and not (n == 1 and u == 1):
                                    pe.wait_ge(sums_out, g)
                                    pe.wait_ge(values_out, values_count(g - 1))
                                    if n == 2 and u == 0:
                                        pe.wait_ge(joined, 4)
                            wait_probs(pe, i)
                            j, pair = s // (L.kt // 2), s % (L.kt // 2)
                            rows = slice(32 * j, 32 * j + 32)
                            for a in tiles:
                                kt = 2 * pair + a
                                first, final = kt == 0, kt == L.kt - 1
                                p_ = pt[:, i % PTB, a, :]
                                if n == 1:
                                    last = nc.tensor.matmul((num, den)[u % 2][rows, :],
                                                            vone[:, kt, u // 2, u % 2 * 32:u % 2 * 32 + 32], p_,
                                                            start=first, stop=final)
                                else:
                                    f0 = u * P + 32 * j
                                    nc.tensor.matmul(num[rows, :], v[:, kt, f0:f0 + 32], p_, start=first, stop=final)
                                    last = nc.tensor.matmul(den[rows, :], ones[:, :], p_, start=first, stop=final)
                            if kind == "pv":
                                last.then_inc(pv_done, 1)
                        elif kind == "o":
                            t = step[2]
                            need_weight(n, "o")
                            o = take_ring(step)
                            wt = w_ap(n, "o")
                            for c in range(NC):
                                if t == 0:
                                    pe.wait_ge(at_done, at_count(unit_at(n, 2 * c + 1 if n == 1 else c)))
                                last = nc.tensor.matmul(o[:, :], at[:, c, t * P:(t + 1) * P], wt[:, c, :],
                                                        start=(c == 0), stop=(c == NC - 1))
                            last.then_inc(ring_full, 1)
                        elif kind == "up":
                            f, m = step[2:]
                            need_weight(n, f"up{f}")
                            wait_moved(pe, ("xT", n, "mid", NC - 1))
                            last = project_T(step, n, f"up{f}", (m * P, (m + 1) * P), xT)
                            last.then_inc(ring_full, 1)
                        elif kind == "down":
                            f = step[2]
                            need_weight(n, f"down{f}")
                            wait_moved(pe, ("up", n, f, NC - 1))
                            if f == 0:
                                wait_probs(pe, SINDEX[("score", n, L.units - 1, L.slots - 1)])
                            wt = w_ap(n, f"down{f}")
                            for t in range(NT):
                                for m in range(NC):
                                    last = nc.tensor.matmul(score_banks[:, t, :], wide[:, f % 2, m, t * P:(t + 1) * P], wt[:, m, :],
                                                            start=(f == 0 and m == 0), stop=(f == NFB - 1 and m == NC - 1))
                                if f == NFB - 1 and t < NT - 1:
                                    last.then_inc(down_done, 1)
                            last.then_inc(down_done, 1)

                @block.scalar
                def _(act):
                    for step in STEPS:
                        kind, n = step[0], step[1] if len(step) > 1 else None
                        L = LAYERS[n] if n in (0, 1, 2, 3) else None
                        if kind == "ctxT":
                            wait_ring_full(act, step)
                            nc.scalar.activation(ctxT[:, step[1], :], ring_bank(step)[:, :], ACT.Copy).then_inc(free_of(step), 1)
                        elif kind == "v" and n == 2:
                            t = step[2]
                            wait_ring_full(act, step)
                            if t == 0:
                                act.wait_ge(keymask_set, 1)
                            nc.scalar.activation(v[:, t, :], ring_bank(step)[:, :], ACT.Identity, bias=0.0,
                                                 scale=mcolk[:, t:t + 1]).then_inc(free_of(step), 1)
                        elif kind in ("xT", "aT"):
                            c = step[-1]
                            wait_ring_full(act, step)
                            dst = xT[:, c, :] if kind == "xT" else wide[:, 0, c, :]
                            if kind == "aT":
                                sc, bi = bias["w2"][:, c:c + 1], bias["b2"][:, c:c + 1]
                                act.wait_ge(pv_done, last_pv(unit_at(1, 7)))
                            elif step[2] == "z":
                                sc, bi = bias["w10"][:, c:c + 1], bias["b10"][:, c:c + 1]
                            elif step[2] == "mid" and n == 0:
                                sc, bi = bias["w20"][:, c:c + 1], bias["b20"][:, c:c + 1]
                            elif step[2] == "mid":
                                sc, bi = bias["w3"][:, c:c + 1], 0.0
                            else:
                                sc, bi = 1.0, 0.0
                            fn = ACT.Copy if kind == "xT" and step[2] == "x" else ACT.Identity
                            ins = nc.scalar.activation(dst, ring_bank(step)[:, :], fn, bias=bi, scale=sc)
                            ins.then_inc(free_of(step), 1)
                        elif kind in ("q", "k"):
                            u = step[2]
                            full, high = parts[kind]
                            wait_ring_full(act, step)
                            former = [s for s in STEPS if s[0] == kind]
                            here = former.index(step)
                            if here:
                                f = former[here - 1]
                                act.wait_ge(split_stacked[kind], stack_count(kind, f[1], f[2], f[3] if kind == "k" else 0))
                            if n == 2:
                                ins = nc.scalar.activation(full[:, :], ring_bank(step)[:, :], ACT.Copy)
                            elif (kind, n) == ("q", 1):
                                ins = nc.scalar.activation(full[:, :], ring_bank(step)[:, :], ACT.Identity,
                                                           bias=bq4[:, u:u + 1], scale=-0.25)
                            else:
                                ins = nc.scalar.activation(full[:, :], ring_bank(step)[:, :], ACT.Identity,
                                                           bias=bias[f"{kind}{n}"][:, u:u + 1])
                            ins.then_inc(free_of(step), 1)
                            act.wait_ge(free_of(step), RINDEX[step] // RING + 1)
                            nc.scalar.activation(high[:, :].bitcast(F32R), full[:, :], ACT.Copy).then_inc(hi_done, 1)
                        elif kind == "max" and n == 1:
                            _, _, u, j, t, _ = step
                            act.wait_ge(free_of(step), RINDEX[step] // RING + 1)
                            nc.scalar.activation(pq[j % 2][:, t, :], pq[j % 2][:, t, :], ACT.Exp, scale=-1.0,
                                                 bias=mcol[:, unit_at(1, u) % 2, 0, 4 * j + t:4 * j + t + 1]
                                                 ).then_inc(exp1_done, 1)
                        elif kind == "score" and not BY_VECTOR[SINDEX[step]]:
                            i = SINDEX[step]
                            act.wait_ge(score_full, i + 1)
                            if i >= PTB:
                                act.wait_ge(pv_done, i - PTB + 1)
                            nc.scalar.activation(pt[:, i % PTB], score_banks[:, 2 * (i % 2):2 * (i % 2) + 2, :],
                                                 ACT.Copy if n == 1 else ACT.Exp, scale=L.scale).then_inc(exp_done, 1)
                        elif kind == "heads" and n == 1:
                            u = step[2]
                            if u % 2 == 0:
                                act.wait_ge(pv_done, last_pv(unit_at(1, u)))
                                nc.scalar.activation(at[:, u // 2, :], num[:, :], ACT.Identity, bias=0.0, scale=lanes[:, 0:1]
                                                     ).then_inc(values1_out, 1)
                        elif kind == "heads":
                            g = unit_at(n, step[2])
                            act.wait_ge(pv_done, last_pv(g))
                            nc.scalar.activation(at[:, step[2], :], num[:, :], ACT.Copy).then_inc(values_out, 1)
                        elif kind == "up":
                            f, m = step[2:]
                            wait_ring_full(act, step)
                            if f >= 2:
                                act.wait_ge(down_done, N_DOWN[("down", n, f - 2)])
                            nc.scalar.activation(wide[:, f % 2, m, :], ring_bank(step)[:, :], ACT.Gelu_apprx_tanh,
                                                 bias=bup[n][:, f * NC + m:f * NC + m + 1]).then_inc(free_of(step), 1)

                @block.vector
                def _(dve):
                    steps = [0]

                    def own(ins):
                        steps[0] += 1
                        ins.then_inc(by_vector, 1)
                        dve.wait_ge(by_vector, steps[0])

                    dve.wait_ge(keymask_in, 48)
                    own(nc.vector.tensor_scalar(mtmp, m8[:, :], 0.0, 1.0, ALU.not_equal, ALU.subtract))
                    own(nc.vector.tensor_scalar(krow[0], mtmp, -MASKED, None, ALU.mult))
                    own(nc.vector.tensor_scalar(mtmp, m32, 0.0, 1.0, ALU.not_equal, ALU.subtract))
                    own(nc.vector.tensor_scalar(krow[1], mtmp, -MASKED, None, ALU.mult))
                    nc.vector.tensor_scalar(mcolk[:, :], m8c[:, :], 0.0, None, ALU.not_equal).then_inc(keymask_set, 1)

                    def row_stats(src, t):
                        own(nc.vector.bn_stats(stats[:, t, :], src[:, t, :]))
                        own(nc.vector.bn_aggr(mv[:, t, :], stats[:, t, :]))

                    def norm(step):
                        _, n, what = step
                        eps = LAYERS[n].eps
                        if what == "ctx":
                            dve.wait_ge(ctx_in, 32)
                        if what == "x":
                            dve.wait_ge(x_in, 16)
                        if what == "out":
                            dve.wait_ge(gamma_in, 32)
                        src = cx if what == "ctx" else (v if (n, what) == (3, "mid") else x)
                        dst = {"out": x, "ctx": cx}.get(what, zrow)
                        if what in ("x", "ctx"):
                            for t in range(NT):
                                row_stats(src, t)
                        if n == 3:
                            own(nc.vector.tensor_tensor(var[:, :], mv[:, :, 0], mv[:, :, 0], ALU.mult))
                            own(nc.vector.tensor_tensor(var[:, :], var[:, :], mv[:, :, 1], ALU.add))
                            nc.vector.tensor_scalar(var[:, :], var[:, :], eps, None, ALU.add).then_inc(var_done, 1)
                        else:
                            nc.vector.tensor_scalar(var[:, :], mv[:, :, 1], eps, None, ALU.add).then_inc(var_done, 1)
                        dve.wait_ge(rstd_done, N_NORM[step])
                        for t in range(NT):
                            if n == 3:
                                ins = nc.vector.tensor_scalar(dst[:, t, :], src[:, t, :], rstd[:, t:t + 1], None, ALU.mult)
                            else:
                                ins = nc.vector.tensor_scalar(dst[:, t, :], src[:, t, :], mv[:, t, 0:1], rstd[:, t:t + 1],
                                                              ALU.subtract, ALU.mult)
                            own(ins)
                            if n == 1:
                                own(nc.vector.tensor_tensor(x[:, t, :], x[:, t, :], row["gamma1"][:, :], ALU.mult))
                                own(nc.vector.tensor_tensor(x[:, t, :], x[:, t, :], row["beta1"][:, :], ALU.add))
                        dve.sem_inc(norm_done, 1)

                    for step in STEPS:
                        kind, n = step[0], step[1] if len(step) > 1 else None
                        L = LAYERS[n] if n in (0, 1, 2, 3) else None
                        if kind in RINGED:
                            bank = ring_bank(step)
                        if kind == "norm":
                            norm(step)
                        elif kind == "v" and n != 2:
                            t = step[2]
                            wait_ring_full(dve, step)
                            if n == 1:
                                ins = nc.vector.tensor_tensor(vone[:, t].rearrange("p g (a d) -> p g a d", d=16)[:, :, 0:4:3],
                                                              bank[:, 0:128].rearrange("p (g a d) -> p g a d", g=4, a=2),
                                                              row["v1"][:, :].rearrange("p (g a d) -> p g a d", g=4, a=2),
                                                              ALU.add)
                            else:
                                ins = nc.vector.tensor_tensor(v[:, t, :], bank[:, :], row[f"v{n}"][:, :], ALU.add)
                            ins.then_inc(free_of(step), 1)
                        elif kind == "max":
                            u, j, t, h = step[2:]
                            g = unit_at(n, u)
                            wait_ring_full(dve, step)
                            col = mcol[:, g % 2, h, 4 * j + t:4 * j + t + 1]
                            if n == 1:
                                if (u, j, t) == (0, 0, 0):
                                    dve.wait_ge(mask_negated, 1)
                                h = 4 * u + j
                                if h >= 2:
                                    dve.wait_ge(score_full, SINDEX[("score", 1, (h - 2) // 4, 2 * ((h - 2) % 4) + 1)] + 1)
                                nc.vector.tensor_tensor_reduce(pq[j % 2][:, t, :], bank[:, :], wide[:, 0, t, :], 1.0, -LOWEST,
                                                               ALU.add, ALU.min, col).then_inc(free_of(step), 1)
                                continue
                            ins = nc.vector.tensor_reduce(col, bank[:, :], AX.X, ALU.max)
                            ins.then_inc(free_of(step), 1)
                            if L.halves == 2 and (j, t, h) == (3, NT - 1, 1):
                                wait_moved(dve, step)
                                nc.vector.tensor_tensor(mcol[:, g % 2, 0, :], mcol[:, g % 2, 0, :],
                                                        mcol[:, g % 2, 1, :], ALU.max).then_inc(max_done, 1)
                        elif kind == "maxT":
                            g = unit_at(n, step[2])
                            wait_ring_full(dve, step)
                            if g:
                                dve.wait_ge(mrow_in, 32 * values_count(g - 1))
                            own(nc.vector.tensor_scalar(nm_hi[:, :], bank[0:16, 0:P], -1.0, None, ALU.mult))
                            nc.vector.scalar_tensor_tensor(out=nm_lo[:, :], in0=bank[0:16, 0:P], scalar=-1.0,
                                                           in1=nm_hi[:, :].bitcast(F32), op0=ALU.mult, op1=ALU.subtract
                                                           ).then_inc(free_of(step), 1)
                        elif kind == "score" and BY_VECTOR[SINDEX[step]]:
                            i = SINDEX[step]
                            dve.wait_ge(score_full, i + 1)
                            dve.wait_ge(pv_done, i - PTB + 1)
                            nc.vector.tensor_copy(pt[:, i % PTB], score_banks[:, 2 * (i % 2):2 * (i % 2) + 2, :]
                                                  ).then_inc(copied, 1)
                        elif kind == "heads":
                            u = step[2]
                            g = unit_at(n, u)
                            dve.wait_ge(pv_done, last_pv(g))
                            if g:
                                dve.wait_ge(rden_done, at_count(g - 1))
                            if n == 1 and u % 2 == 0:
                                dve.wait_ge(values1_out, u // 2 + 1)
                            sums = (num, den)[u % 2] if n == 1 else den
                            nc.vector.transpose(denT[:, :], sums[:, :]).then_inc(sums_out, 1)
                            dve.wait_ge(sums_out, g + 1)
                            if n == 1:
                                first = 16 if u % 2 == 0 else 0
                                own(nc.vector.reciprocal(rec1[:, :, u % 2], denT[:, first:S:32]))
                                if u % 2 == 0:
                                    continue
                                nc.vector.scalar_tensor_tensor(out=at[:, u // 2, :], in0=den[:, :], scalar=lanes[:, 1:2],
                                                               in1=at[:, u // 2, :], op0=ALU.mult, op1=ALU.add
                                                               ).then_inc(joined, 1)
                                columns = rec1[:, :, :].rearrange("p a (g o) -> p a g o", o=1).broadcast_to([P, S // 32, 2, 16])
                            else:
                                own(nc.vector.reciprocal(denT[:, 0:S:32], denT[:, 0:S:32]))
                                columns = denT[:, 0:S:32].rearrange("p (a o) -> p a o", o=1).broadcast_to([P, S // 32, 32])
                            if g:
                                dve.wait_ge(at_done, at_count(g - 1))
                            nc.vector.transpose(rden[:, :], columns).then_inc(rden_done, 1)
                        elif kind == "o":
                            t = step[2]
                            wait_ring_full(dve, step)
                            if n == 2:
                                ins = nc.vector.scalar_tensor_tensor(out=x[:, t, :], in0=bank[:, :], scalar=gtanh[:, 0:1],
                                                                     in1=x[:, t, :], op0=ALU.mult, op1=ALU.add)
                            else:
                                dst = v[:, t, :] if n == 3 else x[:, t, :]
                                own(nc.vector.tensor_tensor(bank[:, :], bank[:, :], row[f"o{n}"][:, :], ALU.add))
                                ins = nc.vector.tensor_tensor(dst, bank[:, :], x[:, t, :], ALU.add)
                            ins.then_inc(free_of(step), 1)
                            if n != 2:
                                wait_moved(dve, step)
                                row_stats(v if n == 3 else x, t)
                        elif kind == "mlp_out":
                            for t in range(NT):
                                dve.wait_ge(down_done, N_DOWN[("down", n, NFB - 1)] - (NT - 1 - t))
                                own(nc.vector.tensor_tensor(score_banks[:, t, :], score_banks[:, t, :], row[f"down{n}"][:, :], ALU.add))
                                nc.vector.tensor_tensor(x[:, t, :], score_banks[:, t, :], x[:, t, :], ALU.add
                                                        ).then_inc(mlp_done, 1)
            for s in sems:
                nc.sync.sem_clear(s)
            nc.all_engine_barrier()


_F32 = ["x", "ctx_2048", "mask_Bx1xSxS2_ff0"]
_VECS = ["L0_xattn_ln1_w", "L0_xattn_ln1_b", "L0_xattn_q_b", "L0_xattn_k_b", "L0_xattn_v_b", "L0_xattn_cproj_b",
         "L0_xattn_ln2_w", "L0_xattn_ln2_b", "L0_xattn_fc_b", "L0_xattn_proj_b", "L1_xattn_bq", "L1_xattn_bk",
         "L1_xattn_bv", "L1_xattn_bo", "L1_xattn_gamma", "L1_xattn_beta", "L2_xattn_ln_gamma",
         "L2_xattn_ln_beta", "L2_xattn_gate", "L3_xattn_q_b", "L3_xattn_out_b", "L3_xattn_postnorm_w",
         "L3_xattn_mlp_b1", "L3_xattn_mlp_b2"]
_BY_PARTITION = ["L0_xattn_q_b", "L0_xattn_k_b", "L3_xattn_q_b", "L3_k_b", "L1_xattn_bq", "L1_xattn_bk",
                 "L0_xattn_ln1_w", "L0_xattn_ln1_b", "L0_xattn_ln2_w", "L0_xattn_ln2_b", "L2_xattn_ln_gamma",
                 "L2_xattn_ln_beta", "L3_xattn_postnorm_w", "L0_xattn_fc_b", "L3_xattn_mlp_b1"]
_WEIGHTS = {"q0": "L0_xattn_q_w", "k0": "L0_xattn_k_w", "v0": "L0_xattn_v_w", "o0": "L0_xattn_cproj_w",
            "up0": "L0_xattn_fc_w", "down0": "L0_xattn_proj_w", "q1": "L1_xattn_Wq", "k1": "L1_xattn_Wk",
            "v1": "L1_xattn_Wv", "o1": "L1_xattn_Wo", "q3": "L3_xattn_q_w", "o3": "L3_xattn_out_w",
            "up3": "L3_xattn_mlp_w1", "down3": "L3_xattn_mlp_w2"}


def kernel(**inputs):
    import numpy as np
    import concourse.bacc as bacc
    from concourse.bass_utils import run_bass_kernel_spmd as run

    a = {k: np.ascontiguousarray(inputs[k]) for k in _F32 + _VECS + ["mask_BxS2_ik0"]}
    a["mask8"] = np.ascontiguousarray(inputs["mask_BxS2_bf1"]).view(np.uint8)
    a["mask8_cols"] = np.ascontiguousarray(a["mask8"].reshape(B, NT, P).transpose(0, 2, 1))
    for k, name in _WEIGHTS.items():
        a[k] = np.ascontiguousarray(inputs[name])
    for k, name in (("q2", "L2_xattn_Wq"), ("k2", "L2_xattn_Wk"), ("v2", "L2_xattn_Wv"), ("o2", "L2_xattn_Wo")):
        a[k] = np.ascontiguousarray(np.asarray(inputs[name]).T)
    kv_w, kv_b = np.asarray(inputs["L3_xattn_kv_w"]), np.asarray(inputs["L3_xattn_kv_b"])
    a["k3"], a["v3"] = np.ascontiguousarray(kv_w[:, 0::2]), np.ascontiguousarray(kv_w[:, 1::2])
    a["L3_k_b"], a["L3_v_b"] = np.ascontiguousarray(kv_b[0::2]), np.ascontiguousarray(kv_b[1::2])

    a["q1"] = np.ascontiguousarray(a["q1"].reshape(D, 4, 8, 16).transpose(0, 1, 3, 2).reshape(D, D))
    a["L1_xattn_bq"] = np.ascontiguousarray(a["L1_xattn_bq"].reshape(4, 8, 16).transpose(0, 2, 1).reshape(D))
    a["k1"] = np.ascontiguousarray(a["k1"].reshape(D, 8, 16).transpose(0, 2, 1).reshape(D, P))
    a["L1_xattn_bk"] = np.ascontiguousarray(a["L1_xattn_bk"].reshape(8, 16).T.reshape(P))
    a["o1"] = np.ascontiguousarray(a["o1"].reshape(4, 2, 4, 16, D).transpose(0, 2, 1, 3, 4).reshape(D, D))
    a["lanes"] = np.stack([np.arange(P) % 32 < 16, np.arange(P) % 32 >= 16], axis=1).astype(np.float32)

    for k in ("q0", "k0", "q2", "k2", "q3", "k3"):
        a[k] = np.ascontiguousarray(a[k].reshape(D, 4, 4, 32).transpose(0, 1, 3, 2).reshape(D, D))
    for k in ("L0_xattn_q_b", "L0_xattn_k_b", "L3_xattn_q_b", "L3_k_b"):
        a[k] = np.ascontiguousarray(a[k].reshape(4, 4, 32).transpose(0, 2, 1).reshape(D))

    for k in _BY_PARTITION:
        a[k] = np.ascontiguousarray(a[k].reshape(-1, P).T)

    nc = bacc.Bacc("TRN2", target_bir_lowering=False, num_devices=1)
    arrays, args = {}, {}
    for k, arr in a.items():
        arrays[f"in_{k}"] = arr
        args[k] = nc.dram_tensor(f"in_{k}", arr.shape, mybir.dt.from_np(arr.dtype), kind="ExternalInput").ap()
    out = nc.dram_tensor("out_0", (B, S, D), F32, kind="ExternalOutput").ap()
    build(nc, args, out)
    r = run(nc, [arrays], core_ids=[0])
    return r.results[0]["out_0"]
```
